# Optimizing a Trainium2 kernel written in Bass

```python
import numpy as np
import jax
import jax.numpy as jnp

def _softmax(x, axis=-1):
    return jax.nn.softmax(x, axis=axis)

def _gelu(x):
    return jax.nn.gelu(x, approximate=True)

def _silu(x):
    return jax.nn.silu(x)

def _sigmoid(x):
    return jax.nn.sigmoid(x)

def _layernorm(x, axis=-1, eps=1e-05):
    m = jnp.mean(x, axis=axis, keepdims=True)
    v = jnp.var(x, axis=axis, keepdims=True)
    return (x - m) / jnp.sqrt(v + eps)

def _scatter_add(tgt, idx, src, axis=0):
    return tgt.at[idx].add(src)

def _segment_sum(src, seg, n):
    return jax.ops.segment_sum(src, seg, n)
kernel_name = 'mk_cond_seq_d1_seqx_r4_dcbb06'

def setup_inputs(seed: int=0):
    np.random.seed(seed)
    _w = jnp.asarray

    def _rec_inputs():
        import jax
        import jax.numpy as jnp
        _rk = jax.random.key(seed)
        x = -0.0002928 + 1 * jax.random.normal(jax.random.fold_in(_rk, 1), (4, 512, 256), jnp.float32)
        _lenS = 512 - jax.random.randint(jax.random.fold_in(_rk, 7), (4,), 0, max(1, 512 // 4) + 1, jnp.int32)
        _lenS2 = 512 - jax.random.randint(jax.random.fold_in(_rk, 8), (4,), 0, max(1, 512 // 4) + 1, jnp.int32)
        cond_2048 = 0.0061147 + 1.02565 * jax.random.normal(jax.random.fold_in(_rk, 11), (4, 512), jnp.float32)
        return (x, cond_2048)
    x, cond_2048 = _rec_inputs()

    def _L0_cond_setup():
        import jax, jax.numpy as jnp
        import numpy as np
        D = 256
        DI = 512
        N = 16
        DT_RANK = 64
        D_CONV = 4
        EPS = 1e-05

        def _layernorm(x, g, b):
            mu = jnp.mean(x, axis=-1, keepdims=True)
            var = jnp.mean((x - mu) ** 2, axis=-1, keepdims=True)
            return (x - mu) * jax.lax.rsqrt(var + EPS) * g + b

        def _mamba(xn, in_proj_w, conv_w, conv_b, x_proj_w, dt_proj_w, dt_proj_b, A_log, D_param, out_proj_w):
            b, sl, _ = xn.shape
            xz = jnp.einsum('bsd,ed->bse', xn, in_proj_w)
            x_in, z = jnp.split(xz, 2, axis=-1)
            xt = jnp.transpose(x_in, (0, 2, 1))
            u = jax.lax.conv_general_dilated(xt, conv_w[:, None, :], (1,), [(D_CONV - 1, 0)], feature_group_count=DI, dimension_numbers=('NCH', 'OIH', 'NCH')) + conv_b[None, :, None]
            u = jax.nn.silu(jnp.transpose(u, (0, 2, 1)))
            x_dbl = jnp.einsum('bsd,ed->bse', u, x_proj_w)
            dt_r, B, C = jnp.split(x_dbl, [DT_RANK, DT_RANK + N], axis=-1)
            dt = jax.nn.softplus(jnp.einsum('bsr,dr->bsd', dt_r, dt_proj_w) + dt_proj_b)
            A = -jnp.exp(A_log)

            def step(h, inp):
                dt_t, B_t, C_t, u_t = inp
                dA = jnp.exp(dt_t[:, :, None] * A)
                h = h * dA + (dt_t * u_t)[:, :, None] * B_t[:, None, :]
                y = jnp.einsum('bdn,bn->bd', h, C_t)
                return (h, y)
            seq = (jnp.transpose(dt, (1, 0, 2)), jnp.transpose(B, (1, 0, 2)), jnp.transpose(C, (1, 0, 2)), jnp.transpose(u, (1, 0, 2)))
            h0 = jnp.zeros((b, DI, N), xn.dtype)
            _, ys = jax.lax.scan(step, h0, seq)
            y = jnp.transpose(ys, (1, 0, 2)) + u * D_param
            y = y * jax.nn.silu(z)
            return jnp.einsum('bsd,ed->bse', y, out_proj_w)
        key = jax.random.key(seed)
        ks = jax.random.split(key, 16)
        s = lambda fan: 1.0 / np.sqrt(fan)
        inp = {'x': jax.random.normal(ks[0], (2, 512, D), jnp.float32), 'c': jax.random.normal(ks[1], (2, 2 * D), jnp.float32), 'ln_g': jnp.ones((D,), jnp.float32), 'ln_b': jnp.zeros((D,), jnp.float32), 'ada_w': jax.random.normal(ks[2], (3 * D, 2 * D), jnp.float32) * s(2 * D), 'ada_b': jnp.zeros((3 * D,), jnp.float32), 'in_proj_w': jax.random.normal(ks[3], (2 * DI, D), jnp.float32) * s(D), 'conv_w': jax.random.normal(ks[4], (DI, D_CONV), jnp.float32) * s(D_CONV), 'conv_b': jnp.zeros((DI,), jnp.float32), 'x_proj_w': jax.random.normal(ks[5], (DT_RANK + 2 * N, DI), jnp.float32) * s(DI), 'dt_proj_w': jax.random.normal(ks[6], (DI, DT_RANK), jnp.float32) * s(DT_RANK), 'dt_proj_b': jax.random.uniform(ks[7], (DI,), jnp.float32, -4.0, -2.0), 'A_log': jnp.tile(jnp.log(jnp.arange(1, N + 1, dtype=jnp.float32)), (DI, 1)), 'D_param': jnp.ones((DI,), jnp.float32), 'out_proj_w': jax.random.normal(ks[8], (D, DI), jnp.float32) * s(DI)}
        return inp
    _L0_cond_all = _L0_cond_setup()
    _L0_cond_in = {k: v for k, v in _L0_cond_all.items() if k in ('ln_g', 'ln_b', 'ada_w', 'ada_b', 'in_proj_w', 'conv_w', 'conv_b', 'x_proj_w', 'dt_proj_w', 'dt_proj_b', 'A_log', 'D_param', 'out_proj_w')}
    del _L0_cond_all
    return {'x': x, 'cond_2048': cond_2048, 'L0_cond_ln_g': _L0_cond_in['ln_g'], 'L0_cond_ln_b': _L0_cond_in['ln_b'], 'L0_cond_ada_w': _L0_cond_in['ada_w'], 'L0_cond_ada_b': _L0_cond_in['ada_b'], 'L0_cond_in_proj_w': _L0_cond_in['in_proj_w'], 'L0_cond_conv_w': _L0_cond_in['conv_w'], 'L0_cond_conv_b': _L0_cond_in['conv_b'], 'L0_cond_x_proj_w': _L0_cond_in['x_proj_w'], 'L0_cond_dt_proj_w': _L0_cond_in['dt_proj_w'], 'L0_cond_dt_proj_b': _L0_cond_in['dt_proj_b'], 'L0_cond_A_log': _L0_cond_in['A_log'], 'L0_cond_D_param': _L0_cond_in['D_param'], 'L0_cond_out_proj_w': _L0_cond_in['out_proj_w']}

def reference(x, cond_2048, L0_cond_ln_g, L0_cond_ln_b, L0_cond_ada_w, L0_cond_ada_b, L0_cond_in_proj_w, L0_cond_conv_w, L0_cond_conv_b, L0_cond_x_proj_w, L0_cond_dt_proj_w, L0_cond_dt_proj_b, L0_cond_A_log, L0_cond_D_param, L0_cond_out_proj_w):
    import jax
    import jax.numpy as jnp

    def _L0_cond_ref(x, c, ln_g, ln_b, ada_w, ada_b, in_proj_w, conv_w, conv_b, x_proj_w, dt_proj_w, dt_proj_b, A_log, D_param, out_proj_w):
        import jax, jax.numpy as jnp
        import numpy as np
        D = 256
        DI = 512
        N = 16
        DT_RANK = 64
        D_CONV = 4
        EPS = 1e-05

        def _layernorm(x, g, b):
            mu = jnp.mean(x, axis=-1, keepdims=True)
            var = jnp.mean((x - mu) ** 2, axis=-1, keepdims=True)
            return (x - mu) * jax.lax.rsqrt(var + EPS) * g + b

        def _mamba(xn, in_proj_w, conv_w, conv_b, x_proj_w, dt_proj_w, dt_proj_b, A_log, D_param, out_proj_w):
            b, sl, _ = xn.shape
            xz = jnp.einsum('bsd,ed->bse', xn, in_proj_w)
            x_in, z = jnp.split(xz, 2, axis=-1)
            xt = jnp.transpose(x_in, (0, 2, 1))
            u = jax.lax.conv_general_dilated(xt, conv_w[:, None, :], (1,), [(D_CONV - 1, 0)], feature_group_count=DI, dimension_numbers=('NCH', 'OIH', 'NCH')) + conv_b[None, :, None]
            u = jax.nn.silu(jnp.transpose(u, (0, 2, 1)))
            x_dbl = jnp.einsum('bsd,ed->bse', u, x_proj_w)
            dt_r, B, C = jnp.split(x_dbl, [DT_RANK, DT_RANK + N], axis=-1)
            dt = jax.nn.softplus(jnp.einsum('bsr,dr->bsd', dt_r, dt_proj_w) + dt_proj_b)
            A = -jnp.exp(A_log)

            def step(h, inp):
                dt_t, B_t, C_t, u_t = inp
                dA = jnp.exp(dt_t[:, :, None] * A)
                h = h * dA + (dt_t * u_t)[:, :, None] * B_t[:, None, :]
                y = jnp.einsum('bdn,bn->bd', h, C_t)
                return (h, y)
            seq = (jnp.transpose(dt, (1, 0, 2)), jnp.transpose(B, (1, 0, 2)), jnp.transpose(C, (1, 0, 2)), jnp.transpose(u, (1, 0, 2)))
            h0 = jnp.zeros((b, DI, N), xn.dtype)
            _, ys = jax.lax.scan(step, h0, seq)
            y = jnp.transpose(ys, (1, 0, 2)) + u * D_param
            y = y * jax.nn.silu(z)
            return jnp.einsum('bsd,ed->bse', y, out_proj_w)
        ada = jnp.einsum('bc,ec->be', jax.nn.silu(c), ada_w) + ada_b
        shift, scale, gate = jnp.split(ada, 3, axis=1)
        xn = _layernorm(x, ln_g, ln_b)
        xn = xn * (1.0 + scale[:, None, :]) + shift[:, None, :]
        x_ssm = _mamba(xn, in_proj_w, conv_w, conv_b, x_proj_w, dt_proj_w, dt_proj_b, A_log, D_param, out_proj_w)
        return x + gate[:, None, :] * x_ssm
    x = _L0_cond_ref(x, cond_2048, L0_cond_ln_g, L0_cond_ln_b, L0_cond_ada_w, L0_cond_ada_b, L0_cond_in_proj_w, L0_cond_conv_w, L0_cond_conv_b, L0_cond_x_proj_w, L0_cond_dt_proj_w, L0_cond_dt_proj_b, L0_cond_A_log, L0_cond_D_param, L0_cond_out_proj_w)
    return x

_drawn_inputs = setup_inputs


def setup_inputs(seed=0):
    import zlib

    import numpy as np

    out = dict(_drawn_inputs(seed))
    spreads = {'L0_cond_ln_g': (1.0, 0.2),
     'L0_cond_ln_b': (0.0, 0.1),
     'L0_cond_ada_b': (0.0, 0.1),
     'L0_cond_conv_b': (0.0, 0.1),
     'L0_cond_D_param': (1.0, 0.2)}
    factors = {}
    for name, (base, spread) in spreads.items():
        noise = np.random.default_rng([zlib.crc32(name.encode()), seed]).standard_normal(out[name].shape)
        drawn = base * np.exp(spread * noise) if base else spread * noise
        out[name] = jnp.asarray(drawn.astype(out[name].dtype))
    for name, factor in factors.items():
        out[name] = (out[name] * factor).astype(out[name].dtype)
    return out
```

```python
import concourse.bass as bass
from concourse import mybir
from contextlib import ExitStack


def mamba_block(nc, x_rows, x_cols, c_cols, vectors, ada_w, in_x_w, in_z_w, x_proj_w, dt_proj_w, out_w, out_cols):
    F32 = mybir.dt.float32
    ALU = mybir.AluOpType
    ACT = mybir.ActivationFunctionType

    P = 128
    BATCHES, T, D = x_rows.shape
    DC = D // P
    KT = T // P
    DI = in_x_w.shape[2]
    C = DI // P
    E_DBL = x_proj_w.shape[2]
    R = dt_proj_w.shape[0] - 1
    N = (E_DBL - R) // 2
    TAPS = 4
    CC = c_cols.shape[1]
    EA = ada_w.shape[2] // P
    EPS = 1e-5
    U = N * C

    at = {}
    col = 0
    for name, width in (("ln_g", DC), ("ln_b", DC), ("ada_b", EA), ("conv_w", C * TAPS), ("conv_b", C),
                        ("d_param", C), ("a_log", C * N)):
        at[name] = col
        col += width
    VCOLS = col

    LAG = 3
    RA, RH, RP = 4, 3, LAG + 2
    DVE_V = (3, 7, 11, 15)

    ctx = ExitStack()
    with ctx:
        def sb(name, shape, dt=F32):
            return ctx.enter_context(nc.sbuf_tensor(name, shape, dt))

        def sem(name):
            return ctx.enter_context(nc.semaphore(name))

        vec = sb("vec", [P, VCOLS])
        w_x = sb("w_x", [P, DC, DI])
        w_z = sb("w_z", [P, DC, DI])
        w_xp = sb("w_xp", [P, C, E_DBL])
        w_dt = sb("w_dt", [R + 1, DI])
        w_out = sb("w_out", [P, C, D])
        ident = sb("ident", [P, P])
        v_buf = sb("v_buf", [P, 2, KT, DI])
        w_ada = v_buf[:].rearrange("p a k d -> p (a k d)")[:, 0:CC * EA * P].rearrange("p (c e) -> p c e", c=CC)
        cond = sb("cond", [P, CC, BATCHES])
        cond_s = sb("cond_s", [P, CC, BATCHES])
        ada = sb("ada", [P, EA, BATCHES])
        ln_scale = sb("ln_scale", [P, DC, BATCHES])
        ln_shift = sb("ln_shift", [P, DC, BATCHES])
        a_exp = sb("a_exp", [P, C * N])
        a_neg = sb("a_neg", [P, C * N])
        x_sb = sb("x_sb", [P, 2, KT, D])
        xt_sb = sb("xt_sb", [P, DC, T])
        stats = sb("stats", [P, KT, 6])
        mean_var = sb("mean_var", [P, KT, 2])
        var_eps = sb("var_eps", [P, KT])
        minus_half = sb("minus_half", [P, KT])
        rstd = sb("rstd", [P, KT])
        xh = sb("xh", [P, KT, D])
        xn = sb("xn", [P, DC, T])
        u = sb("u", [P, C, T])
        dt_rank = sb("dt_rank", [R + 1, T])
        bc = sb("bc", [P, T])
        soft = sb("soft", [P, 2, T])
        dt = sb("dt", [P, 2, C, T])
        dtu = sb("dtu", [P, C, T])
        du = u
        dtu_rows = sb("dtu_rows", [P, 2, KT, DI])
        bc_rows = sb("bc_rows", [P, 2, KT, 2 * N])
        z_rows = sb("z_rows", [P, 2, KT, DI])
        c_rep = sb("c_rep", [P, N, T])
        d_a = sb("d_a", [P, RA, T])
        h = sb("h", [P, RH, T])
        prod = sb("prod", [P, RP, T])
        yg = sb("yg", [P, KT, DI])
        yg_cols = sb("yg_cols", [P, C, T])
        o_sb = sb("o_sb", [P, DC, T])

        c_dram = nc.dram_tensor("c_dram", [BATCHES, N, T], F32, kind="Internal").ap()

        y_ps = [ctx.enter_context(nc.psum_tensor(f"y_ps{k}", [P, DI], F32)) for k in range(KT)]
        dbu_ps = [ctx.enter_context(nc.psum_tensor(f"dbu_ps{i}", [P, T], F32)) for i in range(2)]
        work_ps = [ctx.enter_context(nc.psum_tensor(f"work_ps{i}", [P, T], F32)) for i in range(2)]

        loaded_c = sem("loaded_c")
        loaded_ada_w = sem("loaded_ada_w")
        loaded_w = sem("loaded_w")
        loaded_vec = sem("loaded_vec")
        loaded_x = [sem(f"loaded_x{i}") for i in range(2)]
        loaded_xt = sem("loaded_xt")
        c_stored = sem("c_stored")
        c_loaded = [sem(f"c_loaded{n}") for n in range(N)]
        out_stored = sem("out_stored")
        ident_zero = sem("ident_zero")
        ident_ready = sem("ident_ready")
        cond_ready = sem("cond_ready")
        ada_mm = sem("ada_mm")
        mod_step = sem("mod_step")
        mod_ready = sem("mod_ready")
        a_exp_ready = sem("a_exp_ready")
        a_ready = sem("a_ready")
        KINDS = {"xt": DC, "in": C, "z": KT, "xp": 1, "dt": C, "bct": 1, "du": KT, "yt": C, "o": DC}
        made = {k: sem(f"{k}_made") for k in KINDS}
        taken = {k: sem(f"{k}_taken") for k in KINDS}
        dt_ready = taken["dt"]
        ln_step = sem("ln_step")
        rstd_ready = sem("rstd_ready")
        xh_ready = sem("xh_ready")
        tap_ready = sem("tap_ready")
        conv_step = sem("conv_step")
        u_ready = sem("u_ready")
        sp_step = sem("sp_step")
        sp_ready = sem("sp_ready")
        dtu_ready = sem("dtu_ready")
        du_ready = sem("du_ready")
        v_act = sem("v_act")
        v_dve = sem("v_dve")
        da_ready = sem("da_ready")
        dbu_ready = sem("dbu_ready")
        scan_done = sem("scan_done")
        prod_ready = sem("prod_ready")
        sum_done = sem("sum_done")
        gated = sem("gated")

        PRO = ([("ln", 0)] + [("xt", i) for i in range(DC)] + [("in", c) for c in range(C)]
               + [("z", k) for k in range(KT)] + [("silu_u", 0), ("xp", 0), ("bct", 0)]
               + [("dt", c) for c in range(C)] + [("du", k) for k in range(KT)])
        MAIN_AT = {0: [("yt", 0), ("yt", 1), ("ln", 0)], 1: [("yt", 2), ("yt", 3), ("xt", 0), ("xt", 1)],
                   2: [("o", 0), ("in", 0)], 3: [("o", 1), ("in", 1)], 4: [("in", 2)], 5: [("in", 3)],
                   6: [("z", k) for k in range(KT)] + [("silu_u", 0)], 7: [("xp", 0)],
                   8: [("dt", 0), ("bct", 0)], 9: [("dt", 1)], 10: [("dt", 2)], 11: [("dt", 3)],
                   12: [("du", 0), ("du", 1)], 13: [("du", 2), ("du", 3)]}
        EPI = [("yt", c) for c in range(C)] + [("o", i) for i in range(DC)]

        ORDER = [("piece", k, j, 0) for k, j in PRO]
        ORDER.append(("v", 0, 0))
        units = [(b, n, c) for b in range(BATCHES) for n in range(N) for c in range(C)]

        def sums(i):
            b, n, c = units[i]
            if n == 0 and c == 0:
                ORDER.append(("start", b))
            ORDER.append(("sum", b, n, c))
            if n == N - 1 and c == C - 1:
                ORDER.append(("gate", b))

        for i, (b, n, c) in enumerate(units):
            ORDER.append(("unit", b, n, c))
            if i >= LAG:
                sums(i - LAG)
            pieces = MAIN_AT.get(n, []) if c == C - 1 else []
            for k, j in pieces:
                if k in ("yt", "o"):
                    if b > 0:
                        ORDER.append(("piece", k, j, b - 1))
                elif b + 1 < BATCHES:
                    ORDER.append(("piece", k, j, b + 1))
        for i in range(len(units) - LAG, len(units)):
            sums(i)
        ORDER += [("piece", k, j, BATCHES - 1) for k, j in EPI]

        bank_of, before = {}, {}
        last = {0: None, 1: None}
        turn = 0
        for o in ORDER:
            if o[0] == "piece" and o[1] in KINDS:
                key = o[1:]
                bank_of[key], before[key] = turn, last[turn]
                last[turn] = key
                turn ^= 1

        def nth(kind, j, b):
            return b * KINDS[kind] + j + 1

        def unit_no(b, n, c):
            return (b * N + n) * C + c

        def v_count(b, n, on_dve):
            per = len(DVE_V) if on_dve else N - len(DVE_V)
            return b * per + sum((m in DVE_V) == on_dve for m in range(n + 1))

        block = ctx.enter_context(nc.Block())

        @block.sync
        def _(sp):
            sp.dma_start(vec[:], vectors).then_inc(loaded_vec, 16)
            sp.dma_start(cond[:], c_cols).then_inc(loaded_c, 16)
            sp.dma_start(x_sb[:, 0], x_rows[0].rearrange("(k p) d -> p k d", p=P)).then_inc(loaded_x[0], 16)
            sp.dma_start(w_ada, ada_w).then_inc(loaded_ada_w, 16)
            sp.dma_start(w_x[:], in_x_w).then_inc(loaded_w, 16)
            sp.dma_start(w_z[:], in_z_w).then_inc(loaded_w, 16)
            sp.dma_start(w_xp[:], x_proj_w).then_inc(loaded_w, 16)
            sp.dma_start(w_dt[:], dt_proj_w).then_inc(loaded_w, 16)
            sp.dma_start(w_out[:], out_w).then_inc(loaded_w, 16)
            sp.dma_start(x_sb[:, 1], x_rows[1].rearrange("(k p) d -> p k d", p=P)).then_inc(loaded_x[1], 16)
            sp.dma_start(xt_sb[:], x_cols[0].rearrange("(i p) t -> p i t", p=P)).then_inc(loaded_xt, 16)
            for o in ORDER:
                if o[0] == "piece" and o[1] == "xp":
                    b = o[3]
                    sp.wait_ge(taken["xp"], nth("xp", 0, b))
                    sp.dma_start(c_dram[b], bc[R + N:R + 2 * N, :]).then_inc(c_stored, 16)
                    if b + 2 < BATCHES:
                        sp.wait_ge(xh_ready, b + 1)
                        sp.dma_start(x_sb[:, b % 2], x_rows[b + 2].rearrange("(k p) d -> p k d", p=P)).then_inc(loaded_x[b % 2], 16)
                    if b == 0:
                        sp.wait_ge(c_stored, 16)
                        for n in range(N):
                            sp.dma_start(c_rep[:, n, :], c_dram[0, n:n + 1, :].broadcast_to([P, T])).then_inc(c_loaded[n], 16)
                elif o[0] == "unit" and o[3] == C - 1 and o[1] + 1 < BATCHES:
                    b, n = o[1], o[2]
                    if n == N - 1:
                        sp.wait_ge(c_stored, 16 * (b + 2))
                        for m in range(N):
                            sp.wait_ge(prod_ready, unit_no(b, m, C - 1) + 1)
                            sp.dma_start(c_rep[:, m, :], c_dram[b + 1, m:m + 1, :].broadcast_to([P, T])).then_inc(c_loaded[m], 16)
                elif o[0] == "piece" and o[1] == "o":
                    i, b = o[2], o[3]
                    sp.wait_ge(taken["o"], nth("o", i, b))
                    sp.dma_start(out_cols[b, i * P:(i + 1) * P, :], o_sb[:, i, :]).then_inc(out_stored, 16)
                    if i == DC - 1 and b + 1 < BATCHES:
                        sp.dma_start(xt_sb[:], x_cols[b + 1].rearrange("(i p) t -> p i t", p=P)).then_inc(loaded_xt, 16)
            sp.wait_ge(c_stored, 16 * BATCHES)
            sp.wait_ge(out_stored, 16 * DC * BATCHES)

        @block.gpsimd
        def _(pool):
            nc.gpsimd.memset(ident[:], 0.0).then_inc(ident_zero, 1)
            pool.wait_ge(ident_zero, 1)
            nc.gpsimd.affine_select(out=ident[:], in_=ident[:], compare_op=ALU.not_equal, fill=1.0, base=0,
                                    pattern=[[-1, P]], channel_multiplier=1).then_inc(ident_ready, 1)
            nc.gpsimd.memset(minus_half[:], -0.5).then_inc(ident_ready, 1)
            pool.wait_ge(ident_ready, 2)
            nc.gpsimd.memset(dt_rank[R:R + 1, :], 1.0).then_inc(ident_ready, 1)
            pool.wait_ge(ident_ready, 3)
            for o in ORDER:
                if o[0] == "unit":
                    b, n, c = o[1:]
                    i = unit_no(b, n, c)
                    if c == 0:
                        pool.wait_ge(c_loaded[n], 16 * (b + 1))
                    pool.wait_ge(scan_done, i + 1)
                    if i >= RP:
                        pool.wait_ge(sum_done, i - RP + 1)
                    nc.gpsimd.tensor_tensor(prod[:, i % RP, :], h[:, i % RH, :], c_rep[:, n, :], ALU.mult).then_inc(prod_ready, 1)
                elif o[0] == "piece" and o[1] == "ln":
                    b = o[3]
                    pool.wait_ge(ln_step, 3 * b + 3)
                    nc.gpsimd.tensor_tensor(rstd[:], var_eps[:], minus_half[:], ALU.pow).then_inc(rstd_ready, 1)
                elif o[0] == "piece" and o[1] == "dt":
                    c, b = o[2], o[3]
                    pool.wait_ge(dt_ready, nth("dt", c, b))
                    if b > 0:
                        pool.wait_ge(made["du"], nth("du", KT - 1, b - 1))
                    nc.gpsimd.tensor_tensor(dtu[:, c, :], dt[:, b % 2, c, :], u[:, c, :], ALU.mult).then_inc(dtu_ready, 1)

        @block.tensor
        def _(pe):
            pe.wait_ge(ident_ready, 3)
            pe.wait_ge(loaded_ada_w, 16)
            pe.wait_ge(cond_ready, 1)
            for m in range(EA):
                for k in range(CC):
                    last = nc.tensor.matmul(dbu_ps[0][:, m * BATCHES:(m + 1) * BATCHES], lhsT=w_ada[:, k, m * P:(m + 1) * P],
                                            rhs=cond_s[:, k, :], start=(k == 0), stop=(k == CC - 1))
            last.then_inc(ada_mm, 1)
            pe.wait_ge(loaded_w, 16 * 5)

            def piece(kind, j, b):
                if kind not in KINDS:
                    return
                ps = work_ps[bank_of[kind, j, b]]
                was = before[kind, j, b]
                if was is not None:
                    pe.wait_ge(taken[was[0]], nth(*was))
                if kind == "xt":
                    pe.wait_ge(xh_ready, b + 1)
                    for k in range(KT):
                        last = nc.tensor.transpose(ps[:, k * P:(k + 1) * P], xh[:, k, j * P:(j + 1) * P], ident[:])
                elif kind == "in":
                    pe.wait_ge(taken["xt"], nth("xt", DC - 1, b))
                    for i in range(DC):
                        last = nc.tensor.matmul(ps[:], lhsT=w_x[:, i, j * P:(j + 1) * P], rhs=xn[:, i, :],
                                                start=(i == 0), stop=(i == DC - 1))
                elif kind == "z":
                    for i in range(DC):
                        last = nc.tensor.matmul(ps[:], lhsT=xn[:, i, j * P:(j + 1) * P], rhs=w_z[:, i, :],
                                                start=(i == 0), stop=(i == DC - 1))
                elif kind == "xp":
                    pe.wait_ge(u_ready, b + 1)
                    for c in range(C):
                        last = nc.tensor.matmul(ps[0:E_DBL, :], lhsT=w_xp[:, c, :], rhs=u[:, c, :],
                                                start=(c == 0), stop=(c == C - 1))
                elif kind == "dt":
                    pe.wait_ge(taken["xp"], nth("xp", 0, b))
                    last = nc.tensor.matmul(ps[:], lhsT=w_dt[:, j * P:(j + 1) * P], rhs=dt_rank[:], start=True, stop=True)
                elif kind == "bct":
                    pe.wait_ge(taken["xp"], nth("xp", 0, b))
                    for k in range(KT):
                        last = nc.tensor.transpose(ps[:, k * 2 * N:(k + 1) * 2 * N], bc[R:E_DBL, k * P:(k + 1) * P],
                                                   ident[R:E_DBL, R:E_DBL])
                elif kind == "du":
                    pe.wait_ge(dtu_ready, nth("dt", C - 1, b))
                    for c in range(C):
                        last = nc.tensor.transpose(ps[:, c * P:(c + 1) * P], dtu[:, c, j * P:(j + 1) * P], ident[:])
                elif kind == "yt":
                    pe.wait_ge(gated, KT * (b + 1))
                    for k in range(KT):
                        last = nc.tensor.transpose(ps[:, k * P:(k + 1) * P], yg[:, k, j * P:(j + 1) * P], ident[:])
                elif kind == "o":
                    pe.wait_ge(taken["yt"], nth("yt", C - 1, b))
                    for c in range(C):
                        last = nc.tensor.matmul(ps[:], lhsT=w_out[:, c, j * P:(j + 1) * P], rhs=yg_cols[:, c, :],
                                                start=(c == 0), stop=(c == C - 1))
                last.then_inc(made[kind], 1)

            for o in ORDER:
                if o[0] == "piece":
                    piece(*o[1:])
                elif o[0] == "unit":
                    b, n, c = o[1:]
                    i = unit_no(b, n, c)
                    if c == 0:
                        on_dve = n in DVE_V
                        pe.wait_ge(v_dve if on_dve else v_act, v_count(b, n, on_dve))
                    if i == 0:
                        pe.wait_ge(mod_step, 1)
                    if i >= 2:
                        pe.wait_ge(scan_done, i - 1)
                    for k in range(KT):
                        last = nc.tensor.transpose(dbu_ps[i % 2][:, k * P:(k + 1) * P], v_buf[:, n % 2, k, c * P:(c + 1) * P], ident[:])
                    last.then_inc(dbu_ready, 1)
                elif o[0] == "start":
                    b = o[1]
                    pe.wait_ge(du_ready, nth("dt", C - 1, b))
                    if b > 0:
                        pe.wait_ge(gated, KT * b)
                    for k in range(KT):
                        for c in range(C):
                            nc.tensor.matmul(y_ps[k][:, c * P:(c + 1) * P], lhsT=du[:, c, k * P:(k + 1) * P], rhs=ident[:],
                                             is_transpose=True, start=(c == 0), stop=False, skip_group_check=True)
                elif o[0] == "sum":
                    b, n, c = o[1:]
                    i = unit_no(b, n, c)
                    pe.wait_ge(prod_ready, i + 1)
                    for k in range(KT):
                        last = nc.tensor.matmul(y_ps[k][:, c * P:(c + 1) * P], lhsT=prod[:, i % RP, k * P:(k + 1) * P],
                                                rhs=ident[:], is_transpose=True, start=False,
                                                stop=(n == N - 1 and c == C - 1), skip_group_check=True)
                    last.then_inc(sum_done, 1)

        def scale_by_b(eng, done, b, n, k):
            scale = bc_rows[:, b % 2, k, n:n + 1]
            src, dst = dtu_rows[:, b % 2, k, :], v_buf[:, n % 2, k, :]
            if eng is nc.scalar:
                op = nc.scalar.activation(dst, src, ACT.Copy, scale=scale)
            else:
                op = nc.vector.tensor_scalar(dst, src, scale, None, ALU.mult)
            if k == KT - 1:
                op.then_inc(done, 1)

        def next_v(b, n):
            return (b, n + 1) if n + 1 < N else (b + 1, 0)

        @block.scalar
        def _(act):
            act.wait_ge(loaded_c, 16)
            nc.scalar.activation(cond_s[:], cond[:], ACT.Silu).then_inc(cond_ready, 1)
            act.wait_ge(loaded_vec, 16)
            nc.scalar.activation(a_exp[:], vec[:, at["a_log"]:at["a_log"] + C * N], ACT.Exp).then_inc(a_exp_ready, 1)

            def piece(kind, j, b):
                if kind == "silu_u":
                    for c in range(C):
                        act.wait_ge(taken["in"], nth("in", c, b))
                        last = nc.scalar.activation(u[:, c, :], u[:, c, :], ACT.Silu)
                    last.then_inc(u_ready, 1)
                    return
                if kind not in KINDS or kind == "o":
                    return
                ps = work_ps[bank_of[kind, j, b]]
                act.wait_ge(made[kind], nth(kind, j, b))
                if kind == "xt":
                    if b == 0 and j == 0:
                        act.wait_ge(mod_ready, 1)
                    if b > 0:
                        act.wait_ge(made["z"], nth("z", KT - 1, b - 1))
                    nc.scalar.activation(xn[:, j, :], ps[:], ACT.Identity, scale=ln_scale[:, j, b:b + 1],
                                         bias=ln_shift[:, j, b:b + 1]).then_inc(taken["xt"], 1)
                elif kind == "in":
                    if b > 0:
                        act.wait_ge(sum_done, unit_no(b - 1, 0, 0) + 1)
                    w = at["conv_w"] + j * TAPS + TAPS - 1
                    nc.scalar.activation(u[:, j, :], ps[:], ACT.Identity, scale=vec[:, w:w + 1],
                                         bias=vec[:, at["conv_b"] + j:at["conv_b"] + j + 1]).then_inc(tap_ready, 1)
                elif kind == "z":
                    if b >= 2:
                        act.wait_ge(gated, KT * (b - 1))
                    nc.scalar.activation(z_rows[:, b % 2, j, :], ps[:], ACT.Silu).then_inc(taken["z"], 1)
                elif kind == "xp":
                    if b > 0:
                        act.wait_ge(made["dt"], nth("dt", C - 1, b - 1))
                        act.wait_ge(made["bct"], nth("bct", 0, b - 1))
                        act.wait_ge(c_stored, 16 * b)
                    nc.scalar.copy(dt_rank[0:R, :], ps[0:R, :])
                    nc.scalar.copy(bc[R:E_DBL, :], ps[R:E_DBL, :]).then_inc(taken["xp"], 1)
                elif kind == "dt":
                    i = b * C + j
                    if i >= 2:
                        act.wait_ge(dt_ready, i - 1)
                    nc.scalar.activation(soft[:, i % 2, :], ps[:], ACT.Abs).then_inc(sp_step, 1)
                    act.wait_ge(sp_step, 2 * i + 1)
                    nc.scalar.activation(soft[:, i % 2, :], soft[:, i % 2, :], ACT.Exp, scale=-1.0).then_inc(sp_step, 1)
                    act.wait_ge(sp_step, 2 * i + 2)
                    nc.scalar.activation(soft[:, i % 2, :], soft[:, i % 2, :], ACT.Ln, bias=1.0).then_inc(sp_ready, 1)
                elif kind == "bct":
                    if b >= 2:
                        act.wait_ge(v_dve, v_count(b - 2, N - 1, True))
                        act.wait_ge(v_act, v_count(b - 2, N - 1, False))
                    nc.scalar.copy(bc_rows[:, b % 2].rearrange("p k n -> p (k n)"), ps[:, 0:KT * 2 * N]).then_inc(taken["bct"], 1)
                elif kind == "du":
                    if b >= 2:
                        act.wait_ge(v_dve, v_count(b - 2, N - 1, True))
                        act.wait_ge(v_act, v_count(b - 2, N - 1, False))
                    nc.scalar.copy(dtu_rows[:, b % 2, j, :], ps[:]).then_inc(taken["du"], 1)
                elif kind == "yt":
                    if b > 0:
                        act.wait_ge(made["o"], nth("o", DC - 1, b - 1))
                    nc.scalar.copy(yg_cols[:, j, :], ps[:]).then_inc(taken["yt"], 1)

            def v_waits(b, n):
                act.wait_ge(taken["bct"], b + 1)
                act.wait_ge(taken["du"], nth("du", KT - 1, b))
                if b or n > 1:
                    act.wait_ge(dbu_ready, (b * N + n - 1) * C)
                if b == 0 and n < 2:
                    act.wait_ge(ada_mm, 1)

            for o in ORDER:
                if o[0] == "piece":
                    piece(*o[1:])
                elif o[0] == "v":
                    v_waits(0, 0)
                    for k in range(KT):
                        scale_by_b(nc.scalar, v_act, 0, 0, k)
                elif o[0] == "unit":
                    b, n, c = o[1:]
                    i = unit_no(b, n, c)
                    if i == 0:
                        act.wait_ge(a_ready, 1)
                        act.wait_ge(dt_ready, C)
                    if n == 0 and c == 0:
                        act.wait_ge(dt_ready, nth("dt", C - 1, b))
                    if i >= RA:
                        act.wait_ge(scan_done, i - RA + 1)
                    nc.scalar.activation(d_a[:, i % RA, :], dt[:, b % 2, c, :], ACT.Exp,
                                         scale=a_neg[:, c * N + n:c * N + n + 1]).then_inc(da_ready, 1)
                    nb, nn = next_v(b, n)
                    if nb < BATCHES and nn not in DVE_V:
                        if c == 0:
                            v_waits(nb, nn)
                        scale_by_b(nc.scalar, v_act, nb, nn, c)

        @block.vector
        def _(dve):
            dve.wait_ge(loaded_vec, 16)
            dve.wait_ge(ada_mm, 1)
            ab = vec[:, at["ada_b"]:at["ada_b"] + EA].unsqueeze(2).broadcast_to([P, EA, BATCHES])
            nc.vector.tensor_tensor(ada[:], dbu_ps[0][:, 0:EA * BATCHES].rearrange("p (m b) -> p m b", m=EA), ab,
                                    ALU.add).then_inc(mod_step, 1)
            dve.wait_ge(mod_step, 1)
            g = vec[:, at["ln_g"]:at["ln_g"] + DC].unsqueeze(2).broadcast_to([P, DC, BATCHES])
            lb = vec[:, at["ln_b"]:at["ln_b"] + DC].unsqueeze(2).broadcast_to([P, DC, BATCHES])
            scale, shift = ada[:, DC:2 * DC, :], ada[:, 0:DC, :]
            nc.vector.scalar_tensor_tensor(ln_scale[:], scale, 1.0, g, ALU.add, ALU.mult)
            nc.vector.scalar_tensor_tensor(ln_shift[:], scale, 1.0, lb, ALU.add, ALU.mult).then_inc(mod_step, 1)
            dve.wait_ge(mod_step, 2)
            nc.vector.tensor_tensor(ln_shift[:], ln_shift[:], shift, ALU.add).then_inc(mod_ready, 1)
            dve.wait_ge(a_exp_ready, 1)
            nc.vector.tensor_scalar(a_neg[:], a_exp[:], -1.0, None, ALU.mult).then_inc(a_ready, 1)

            def piece(kind, j, b):
                if kind == "ln":
                    dve.wait_ge(loaded_x[b % 2], 16 * (b // 2 + 1))
                    if b > 0:
                        dve.wait_ge(made["xt"], nth("xt", DC - 1, b - 1))
                    for k in range(KT):
                        last = nc.vector.bn_stats(stats[:, k, :], x_sb[:, b % 2, k, :])
                    last.then_inc(ln_step, 1)
                    dve.wait_ge(ln_step, 3 * b + 1)
                    for k in range(KT):
                        last = nc.vector.bn_aggr(mean_var[:, k, :], stats[:, k, :])
                    last.then_inc(ln_step, 1)
                    dve.wait_ge(ln_step, 3 * b + 2)
                    nc.vector.tensor_scalar(var_eps[:], mean_var[:, :, 1], EPS, None, ALU.add).then_inc(ln_step, 1)
                    dve.wait_ge(rstd_ready, b + 1)
                    for k in range(KT):
                        last = nc.vector.tensor_scalar(xh[:, k, :], x_sb[:, b % 2, k, :], mean_var[:, k, 0:1],
                                                       rstd[:, k:k + 1], ALU.subtract, ALU.mult)
                    last.then_inc(xh_ready, 1)
                elif kind == "in":
                    ps = work_ps[bank_of[kind, j, b]]
                    dve.wait_ge(tap_ready, nth("in", j, b))
                    for delay in range(1, TAPS):
                        w = at["conv_w"] + j * TAPS + TAPS - 1 - delay
                        if delay > 1:
                            dve.wait_ge(conv_step, (TAPS - 2) * (b * C + j) + delay - 1)
                        nc.vector.scalar_tensor_tensor(u[:, j, delay:T], ps[:, 0:T - delay], vec[:, w:w + 1], u[:, j, delay:T],
                                                       ALU.mult, ALU.add).then_inc(taken["in"] if delay == TAPS - 1 else conv_step, 1)
                elif kind == "dt":
                    i = b * C + j
                    ps = work_ps[bank_of[kind, j, b]]
                    dve.wait_ge(sp_ready, i + 1)
                    if b >= 2 and j == 0:
                        dve.wait_ge(da_ready, unit_no(b - 2, N - 1, C - 1) + 1)
                    nc.vector.scalar_tensor_tensor(dt[:, b % 2, j, :], ps[:], 0.0, soft[:, i % 2, :], ALU.max,
                                                   ALU.add).then_inc(dt_ready, 1)
                    dve.wait_ge(dtu_ready, i + 1)
                    nc.vector.tensor_scalar(du[:, j, :], u[:, j, :], vec[:, at["d_param"] + j:at["d_param"] + j + 1], None,
                                            ALU.mult).then_inc(du_ready, 1)
                elif kind == "o":
                    ps = work_ps[bank_of[kind, j, b]]
                    dve.wait_ge(made["o"], nth("o", j, b))
                    dve.wait_ge(loaded_xt, 16 * (b + 1))
                    if b > 0:
                        dve.wait_ge(out_stored, 16 * DC * b)
                    nc.vector.scalar_tensor_tensor(o_sb[:, j, :], ps[:], ada[:, 2 * DC + j, b:b + 1], xt_sb[:, j, :],
                                                   ALU.mult, ALU.add).then_inc(taken["o"], 1)

            for o in ORDER:
                if o[0] == "piece":
                    piece(*o[1:])
                elif o[0] == "unit":
                    b, n, c = o[1:]
                    i = unit_no(b, n, c)
                    dve.wait_ge(dbu_ready, i + 1)
                    dve.wait_ge(da_ready, i + 1)
                    if i >= RH:
                        dve.wait_ge(prod_ready, i - RH + 1)
                    nc.vector.tensor_tensor_scan(h[:, i % RH, :], d_a[:, i % RA, :], dbu_ps[i % 2][:], 0.0, ALU.mult,
                                                 ALU.add).then_inc(scan_done, 1)
                    nb, nn = next_v(b, n)
                    if nb < BATCHES and nn in DVE_V:
                        if c == 0:
                            dve.wait_ge(taken["bct"], nb + 1)
                            dve.wait_ge(taken["du"], nth("du", KT - 1, nb))
                            dve.wait_ge(dbu_ready, (nb * N + nn - 1) * C)
                        scale_by_b(nc.vector, v_dve, nb, nn, c)
                elif o[0] == "gate":
                    b = o[1]
                    dve.wait_ge(sum_done, U * (b + 1))
                    if b > 0:
                        dve.wait_ge(made["yt"], nth("yt", C - 1, b - 1))
                    dve.wait_ge(taken["z"], nth("z", KT - 1, b))
                    for k in range(KT):
                        nc.vector.tensor_tensor(yg[:, k, :], y_ps[k][:], z_rows[:, b % 2, k, :], ALU.mult).then_inc(gated, 1)


_INS = ["x_rows", "x_cols", "c_cols", "vectors", "ada_w", "in_x_w", "in_z_w", "x_proj_w", "dt_proj_w", "out_w"]


def kernel(**inputs):
    import numpy as np
    import concourse.bacc as bacc
    from concourse import mybir
    from concourse.bass_utils import run_bass_kernel_spmd

    w = {k.removeprefix("L0_cond_"): np.asarray(v) for k, v in inputs.items()}
    P = 128

    def chunks(a):
        return np.ascontiguousarray(np.moveaxis(a.reshape(a.shape[0] // P, P, *a.shape[1:]), 0, 1))

    x = w["x"]
    DI = w["in_proj_w"].shape[0] // 2
    names = ["ln_g", "ln_b", "ada_b", "conv_w", "conv_b", "D_param", "A_log"]
    laid = {
        "x_rows": x,
        "x_cols": x.transpose(0, 2, 1),
        "c_cols": chunks(w["cond_2048"].T),
        "vectors": np.concatenate([chunks(w[n]).reshape(P, -1) for n in names], axis=1),
        "ada_w": chunks(w["ada_w"].T),
        "in_x_w": chunks(w["in_proj_w"][:DI].T),
        "in_z_w": chunks(w["in_proj_w"][DI:].T),
        "x_proj_w": chunks(w["x_proj_w"].T),
        "dt_proj_w": np.concatenate([w["dt_proj_w"].T, w["dt_proj_b"][None, :]], axis=0),
        "out_w": chunks(w["out_proj_w"].T),
    }
    nc = bacc.Bacc("TRN2", target_bir_lowering=False, num_devices=1)
    arrays, args = {}, []
    for name in _INS:
        a = np.ascontiguousarray(laid[name])
        arrays[f"in_{name}"] = a
        args.append(nc.dram_tensor(f"in_{name}", a.shape, mybir.dt.from_np(a.dtype), kind="ExternalInput").ap())
    B, T, D = x.shape
    args.append(nc.dram_tensor("out_cols", (B, D, T), mybir.dt.float32, kind="ExternalOutput").ap())
    mamba_block(nc, *args)
    r = run_bass_kernel_spmd(nc, [arrays], core_ids=[0])
    return np.ascontiguousarray(r.results[0]["out_cols"].transpose(0, 2, 1))
```

```python
import concourse.bass as bass
from concourse import mybir
from contextlib import ExitStack


def mamba_block(nc, x_rows, x_cols, c_cols, vectors, ada_w, in_x_w, in_z_w, x_proj_w, dt_proj_w, out_w, out_cols):
    F32 = mybir.dt.float32
    ALU = mybir.AluOpType
    ACT = mybir.ActivationFunctionType

    P = 128
    BATCHES, T, D = x_rows.shape
    DC = D // P
    KT = T // P
    DI = in_x_w.shape[2]
    C = DI // P
    E_DBL = x_proj_w.shape[2]
    R = dt_proj_w.shape[0] - 1
    N = (E_DBL - R) // 2
    TAPS = 4
    CC = c_cols.shape[1]
    EA = ada_w.shape[2] // P
    EPS = 1e-5
    U = N * C

    at = {}
    col = 0
    for name, width in (("ln_g", DC), ("ln_b", DC), ("ada_b", EA), ("conv_w", C * TAPS), ("conv_b", C),
                        ("d_param", C), ("a_log", C * N)):
        at[name] = col
        col += width
    VCOLS = col

    LAG = 5
    RA, RH, RP = 4, 4, LAG + 2
    RV, RC = 3, 5
    DVE_V = (7, 9, 12, 14)

    ctx = ExitStack()
    with ctx:
        def sb(name, shape, dt=F32):
            return ctx.enter_context(nc.sbuf_tensor(name, shape, dt))

        def sem(name):
            return ctx.enter_context(nc.semaphore(name))

        vec = sb("vec", [P, VCOLS])
        w_x = sb("w_x", [P, DC, DI])
        w_z = sb("w_z", [P, DC, DI])
        w_xp = sb("w_xp", [P, C, E_DBL])
        w_dt = sb("w_dt", [R + 1, DI])
        w_out = sb("w_out", [P, C, D])
        ident = sb("ident", [P, P])
        v_buf = sb("v_buf", [P, RV, KT, DI])
        w_ada = v_buf[:].rearrange("p a k d -> p (a k d)")[:, 0:CC * EA * P].rearrange("p (c e) -> p c e", c=CC)
        cond = sb("cond", [P, CC, BATCHES])
        cond_s = sb("cond_s", [P, CC, BATCHES])
        ada = sb("ada", [P, EA, BATCHES])
        ln_scale = sb("ln_scale", [P, DC, BATCHES])
        ln_shift = sb("ln_shift", [P, DC, BATCHES])
        a_exp = sb("a_exp", [P, C * N])
        a_neg = sb("a_neg", [P, C * N])
        x_sb = sb("x_sb", [P, 2, KT, D])
        xt_sb = sb("xt_sb", [P, DC, T])
        stats = sb("stats", [P, KT, 6])
        mean_var = sb("mean_var", [P, KT, 2])
        var_eps = sb("var_eps", [P, KT])
        minus_half = sb("minus_half", [P, KT])
        rstd = sb("rstd", [P, KT])
        xh = sb("xh", [P, KT, D])
        xn = sb("xn", [P, 2, DC, T])
        u = sb("u", [P, C, T])
        dt_rank = sb("dt_rank", [R + 1, T])
        bc = sb("bc", [P, T])
        soft = sb("soft", [P, 2, T])
        dt = sb("dt", [P, 2, C, T])
        dtu = sb("dtu", [P, C, T])
        du = u
        dtu_rows = sb("dtu_rows", [P, 2, KT, DI])
        bc_rows = sb("bc_rows", [P, 2, KT, 2 * N])
        z_rows = sb("z_rows", [P, KT, DI])
        c_rep = sb("c_rep", [P, RC, T])
        d_a = sb("d_a", [P, RA, T])
        h = sb("h", [P, RH, T])
        prod = sb("prod", [P, RP, T])
        yg = sb("yg", [P, KT, DI])
        yg_cols = sb("yg_cols", [P, C, T])
        o_sb = sb("o_sb", [P, DC, T])

        c_dram = nc.dram_tensor("c_dram", [BATCHES, N, T], F32, kind="Internal").ap()

        y_ps = [ctx.enter_context(nc.psum_tensor(f"y_ps{k}", [P, DI], F32)) for k in range(KT)]
        dbu_ps = [ctx.enter_context(nc.psum_tensor(f"dbu_ps{i}", [P, T], F32)) for i in range(2)]
        work_ps = [ctx.enter_context(nc.psum_tensor(f"work_ps{i}", [P, T], F32)) for i in range(2)] + y_ps + dbu_ps

        loaded_c = sem("loaded_c")
        loaded_ada_w = sem("loaded_ada_w")
        loaded_w_x = sem("loaded_w_x")
        loaded_w_z = sem("loaded_w_z")
        loaded_w_xp = sem("loaded_w_xp")
        loaded_w_dt = sem("loaded_w_dt")
        loaded_w_out = sem("loaded_w_out")
        loaded_vec = sem("loaded_vec")
        loaded_x = [sem(f"loaded_x{i}") for i in range(2)]
        loaded_xt = sem("loaded_xt")
        c_stored = sem("c_stored")
        c_loaded = [sem(f"c_loaded{i}") for i in range(RC)]
        out_stored = sem("out_stored")
        ident_zero = sem("ident_zero")
        ident_ready = sem("ident_ready")
        cond_ready = sem("cond_ready")
        ada_mm = sem("ada_mm")
        mod_step = sem("mod_step")
        mod_ready = sem("mod_ready")
        a_exp_ready = sem("a_exp_ready")
        a_ready = sem("a_ready")
        KINDS = {"xt": DC, "in": C, "z": KT, "xp": 1, "dt": C, "bct": 1, "du": KT, "yt": KT, "o": KT}
        STEPS = {"in": DC, "z": DC, "xp": C, "o": DC}
        made = {k: sem(f"{k}_made") for k in KINDS}
        taken = {k: sem(f"{k}_taken") for k in KINDS}
        dt_ready = taken["dt"]
        ln_step = sem("ln_step")
        rstd_ready = sem("rstd_ready")
        xh_ready = sem("xh_ready")
        tap_ready = sem("tap_ready")
        conv_step = sem("conv_step")
        u_ready = sem("u_ready")
        sp_step = sem("sp_step")
        sp_ready = sem("sp_ready")
        dtu_ready = sem("dtu_ready")
        du_ready = sem("du_ready")
        v_act = sem("v_act")
        v_dve = sem("v_dve")
        da_ready = sem("da_ready")
        dbu_ready = sem("dbu_ready")
        scan_done = sem("scan_done")
        prod_ready = sem("prod_ready")
        sum_done = sem("sum_done")
        gated = sem("gated")

        order = []

        def put(pos, engine, *what):
            order.append((pos, len(order), engine, what))

        bank_of = {}
        AA = 2

        def put_stage(pos, bank, kind, j, b, behind=(("act", AA),)):
            bank_of[kind, j, b] = work_ps[bank]
            for step in range(STEPS.get(kind, 1)):
                put(pos - (STEPS.get(kind, 1) - 1 - step) * 0.9, "pe", kind, j, b, step)
            for engine, lag in behind:
                put(pos + lag, engine, kind, j, b)

        def prologue(at, b):
            put(at - 8, "dve", "stats", 0, b)
            put(at - 7.5, "pool", "rstd", 0, b)
            put(at - 2, "dve", "xh", 0, b)
            for i in range(DC):
                put_stage(at + i, i % 2, "xt", i, b)
            for c in range(C):
                put_stage(at + 4 + 3.5 * c, c % 2 if b else 2 + c, "in", c, b)
                for delay in range(1, TAPS):
                    put(at + 4 + 3.5 * c + AA + 0.5, "dve", "tap", c, b, delay)
            put(at + 22.4, "act", "silu_table", 0, b)
            put(at + 22.6, "act", "silu_u", 0, b)
            put(at + (22.8 if b else 29.6), "act", "exp_table", 0, b)
            put_stage(at + 25.7, 0, "xp", 0, b, (("act", AA), ("sp", 5)))
            put_stage(at + 29, 1, "bct", 0, b)
            for c in range(C):
                on_pe = at + 29.5 + 3 * c
                put_stage(on_pe, c % 2 if b else 2 + c, "dt", c, b, (("act", AA), ("dve", AA + 1)))
                put(on_pe + AA + 2, "pool" if b else "dve", "dtu", c, b)
                put(at + 54 + c, "dve", "du", c, b)
            for k in range(KT):
                put_stage(at + (49, 52, 52.8, 55.8)[k], k % 2, "du", k, b)

        def z_stage(at, b):
            for k in range(KT):
                if b:
                    put_stage(at + (18, 20.5, 22, 22.3)[k], k % 2, "z", k, b, ())
                    put(at + (22.5 if k < 2 else 22.7), "act", "z", k, b)
                else:
                    put_stage(at + (18, 18.5, 26, 26.5)[k], (0, 1, 7, 6)[k], "z", k, b, ())
                    put(at + (22.65 if k < 2 else 29.5), "act", "z", k, b)
            if b + 1 == BATCHES:
                put(at + 22.4, "act", "silu_table", 0, b)
                put(at + 22.8, "act", "exp_table", 0, b)

        def epilogue(at, b):
            for k in range(KT):
                put_stage(at + (41.5, 44.5, 45, 48)[k], k % 2, "yt", k, b)
                put_stage(at + (59, 60.5, 61.5, 63)[k], k % 2, "o", k, b, (("dve", 1), ("sp", 2)))

        prologue(-U, 0)
        z_stage(-U, 0)
        put(-U + 1.5, "pe", "ada", 0, 0)
        put(-U - 1, "dve", "ada", 0, 0)
        put(-1, "dve", "v", 0, 0)
        for b in range(BATCHES):
            if b + 1 < BATCHES:
                prologue(b * U, b + 1)
            if b > 0:
                z_stage(b * U, b)
                epilogue(b * U, b - 1)
            for n in range(N):
                s = b * N + n
                put(-1 if s < RC else (s - RC + 1) * C + 0.5, "sp", "load_c", b, n)
                for c in range(C):
                    i = s * C + c
                    for engine in ("act", "pe", "dve", "pool"):
                        put(i, engine, "unit", b, n, c)
                    if n == 0 and c == 0:
                        put(i + LAG, "pe", "start", b)
                    put(i + LAG, "pe", "sum", b, n, c)
            put((b + 1) * U - 1 + LAG, "dve", "gate", b)
        epilogue(BATCHES * U, BATCHES - 1)
        order.sort(key=lambda o: o[:2])

        def work_of(engine):
            return [what for _, _, e, what in order if e == engine]

        before = {}
        last = [None] * len(work_ps)
        for what in work_of("pe"):
            if what[0] in KINDS and what[3] == 0:
                key = what[:3]
                bank = work_ps.index(bank_of[key])
                before[key], last[bank] = last[bank], key

        def nth(kind, j, b):
            return b * KINDS[kind] + j + 1

        def unit_no(b, n, c):
            return (b * N + n) * C + c

        def v_on_dve(b, n):
            return n in DVE_V or (b, n) == (0, 0)

        def v_count(b, n, on_dve):
            return sum(v_on_dve(s // N, s % N) == on_dve for s in range(b * N + n + 1))

        block = ctx.enter_context(nc.Block())

        @block.sync
        def _(sp):
            sp.dma_start(x_sb[:, 0], x_rows[0].rearrange("(k p) d -> p k d", p=P)).then_inc(loaded_x[0], 16)
            sp.dma_start(cond[:], c_cols).then_inc(loaded_c, 16)
            sp.dma_start(vec[:], vectors).then_inc(loaded_vec, 16)
            sp.dma_start(w_x[:], in_x_w).then_inc(loaded_w_x, 16)
            sp.dma_start(w_xp[:], x_proj_w).then_inc(loaded_w_xp, 16)
            sp.dma_start(w_dt[:], dt_proj_w).then_inc(loaded_w_dt, 16)
            sp.dma_start(x_sb[:, 1], x_rows[1].rearrange("(k p) d -> p k d", p=P)).then_inc(loaded_x[1], 16)
            sp.dma_start(w_z[:], in_z_w).then_inc(loaded_w_z, 16)
            sp.dma_start(w_out[:], out_w).then_inc(loaded_w_out, 16)
            sp.dma_start(xt_sb[:], x_cols[0].rearrange("(i p) t -> p i t", p=P)).then_inc(loaded_xt, 16)
            for what in work_of("sp"):
                if what[0] == "xp":
                    b = what[2]
                    sp.wait_ge(taken["xp"], b + 1)
                    sp.dma_start(c_dram[b], bc[R + N:R + 2 * N, :]).then_inc(c_stored, 16)
                    if b + 2 < BATCHES:
                        sp.wait_ge(xh_ready, b + 1)
                        sp.dma_start(x_sb[:, b % 2], x_rows[b + 2].rearrange("(k p) d -> p k d", p=P)).then_inc(loaded_x[b % 2], 16)
                elif what[0] == "load_c":
                    b, n = what[1:]
                    s = b * N + n
                    sp.wait_ge(c_stored, 16 * (b + 1))
                    if s >= RC:
                        sp.wait_ge(prod_ready, (s - RC + 1) * C)
                    sp.dma_start(c_rep[:, s % RC, :], c_dram[b, n:n + 1, :].broadcast_to([P, T])).then_inc(c_loaded[s % RC], 16)
                elif what[0] == "o":
                    k, b = what[1:]
                    sp.wait_ge(taken["o"], nth("o", k, b))
                    t = slice(k * P, (k + 1) * P)
                    sp.dma_start(out_cols[b, :, t].rearrange("(i p) t -> p i t", p=P), o_sb[:, :, t]).then_inc(out_stored, 16)
                    if k == KT - 1 and b + 1 < BATCHES:
                        sp.dma_start(xt_sb[:], x_cols[b + 1].rearrange("(i p) t -> p i t", p=P)).then_inc(loaded_xt, 16)
            sp.wait_ge(c_stored, 16 * BATCHES)
            sp.wait_ge(out_stored, 16 * KT * BATCHES)

        @block.gpsimd
        def _(pool):
            nc.gpsimd.memset(ident[:], 0.0).then_inc(ident_zero, 1)
            pool.wait_ge(ident_zero, 1)
            nc.gpsimd.affine_select(out=ident[:], in_=ident[:], compare_op=ALU.not_equal, fill=1.0, base=0,
                                    pattern=[[-1, P]], channel_multiplier=1).then_inc(ident_ready, 1)
            nc.gpsimd.memset(minus_half[:], -0.5).then_inc(ident_ready, 1)
            pool.wait_ge(ident_ready, 2)
            nc.gpsimd.memset(dt_rank[R:R + 1, :], 1.0).then_inc(ident_ready, 1)
            pool.wait_ge(ident_ready, 3)
            for what in work_of("pool"):
                if what[0] == "unit":
                    b, n, c = what[1:]
                    i = unit_no(b, n, c)
                    s = b * N + n
                    if c == 0:
                        pool.wait_ge(c_loaded[s % RC], 16 * (s // RC + 1))
                    pool.wait_ge(scan_done, i + 1)
                    if i >= RP:
                        pool.wait_ge(sum_done, i - RP + 1)
                    nc.gpsimd.tensor_tensor(prod[:, i % RP, :], h[:, i % RH, :], c_rep[:, s % RC, :], ALU.mult).then_inc(prod_ready, 1)
                elif what[0] == "rstd":
                    b = what[2]
                    pool.wait_ge(ln_step, 3 * b + 3)
                    nc.gpsimd.tensor_tensor(rstd[:], var_eps[:], minus_half[:], ALU.pow).then_inc(rstd_ready, 1)
                elif what[0] == "dtu":
                    c, b = what[1:]
                    pool.wait_ge(dt_ready, nth("dt", c, b))
                    if b > 0:
                        pool.wait_ge(made["du"], nth("du", KT - 1, b - 1))
                    nc.gpsimd.tensor_tensor(dtu[:, c, :], dt[:, b % 2, c, :], u[:, c, :], ALU.mult).then_inc(dtu_ready, 1)

        @block.tensor
        def _(pe):
            pe.wait_ge(ident_ready, 3)
            def ada_products(first, last):
                for m in range(first, last):
                    for k in range(CC):
                        op = nc.tensor.matmul(dbu_ps[0][:, m * BATCHES:(m + 1) * BATCHES], lhsT=w_ada[:, k, m * P:(m + 1) * P],
                                              rhs=cond_s[:, k, :], start=(k == 0), stop=(k == CC - 1))
                op.then_inc(ada_mm, 1)

            def stage(kind, j, b, step):
                ps = bank_of[kind, j, b]
                was = before[kind, j, b]
                first, final = step == 0, step == STEPS.get(kind, 1) - 1
                if first and was is not None:
                    pe.wait_ge(taken[was[0]], nth(*was))
                if kind == "xt":
                    pe.wait_ge(xh_ready, b + 1)
                    for k in range(KT):
                        last = nc.tensor.transpose(ps[:, k * P:(k + 1) * P], xh[:, k, j * P:(j + 1) * P], ident[:])
                elif kind == "in":
                    if first:
                        pe.wait_ge(loaded_w_x, 16)
                        pe.wait_ge(taken["xt"], nth("xt", DC - 1, b))
                    last = nc.tensor.matmul(ps[:], lhsT=w_x[:, step, j * P:(j + 1) * P], rhs=xn[:, b % 2, step, :],
                                            start=first, stop=final)
                elif kind == "z":
                    if first:
                        pe.wait_ge(loaded_w_z, 16)
                        if b == 0:
                            pe.wait_ge(mod_step, 1)
                    last = nc.tensor.matmul(ps[:], lhsT=xn[:, b % 2, step, j * P:(j + 1) * P], rhs=w_z[:, step, :],
                                            start=first, stop=final)
                elif kind == "xp":
                    if first:
                        pe.wait_ge(loaded_w_xp, 16)
                        pe.wait_ge(u_ready, b + 1)
                    last = nc.tensor.matmul(ps[0:E_DBL, :], lhsT=w_xp[:, step, :], rhs=u[:, step, :], start=first, stop=final)
                elif kind == "dt":
                    pe.wait_ge(loaded_w_dt, 16)
                    pe.wait_ge(taken["xp"], nth("xp", 0, b))
                    last = nc.tensor.matmul(ps[:], lhsT=w_dt[:, j * P:(j + 1) * P], rhs=dt_rank[:], start=True, stop=True)
                elif kind == "bct":
                    pe.wait_ge(taken["xp"], nth("xp", 0, b))
                    for k in range(KT):
                        last = nc.tensor.transpose(ps[:, k * 2 * N:(k + 1) * 2 * N], bc[R:E_DBL, k * P:(k + 1) * P],
                                                   ident[R:E_DBL, R:E_DBL])
                elif kind == "du":
                    pe.wait_ge(dtu_ready, nth("dt", C - 1, b))
                    for c in range(C):
                        last = nc.tensor.transpose(ps[:, c * P:(c + 1) * P], dtu[:, c, j * P:(j + 1) * P], ident[:])
                elif kind == "yt":
                    pe.wait_ge(gated, nth("yt", j, b))
                    for c in range(C):
                        last = nc.tensor.transpose(ps[:, c * P:(c + 1) * P], yg[:, j, c * P:(c + 1) * P], ident[:])
                elif kind == "o":
                    if first:
                        pe.wait_ge(loaded_w_out, 16)
                        pe.wait_ge(taken["yt"], nth("yt", j, b))
                    for c in range(C):
                        last = nc.tensor.matmul(ps[:, step * P:(step + 1) * P], lhsT=w_out[:, c, step * P:(step + 1) * P],
                                                rhs=yg_cols[:, c, j * P:(j + 1) * P], start=(c == 0), stop=(c == C - 1))
                if final:
                    last.then_inc(made[kind], 1)

            for what in work_of("pe"):
                if what[0] in KINDS:
                    stage(*what)
                elif what[0] == "ada":
                    pe.wait_ge(loaded_ada_w, 16)
                    pe.wait_ge(cond_ready, 1)
                    ada_products(0, EA)
                elif what[0] == "unit":
                    b, n, c = what[1:]
                    i = unit_no(b, n, c)
                    if c == 0:
                        on_dve = v_on_dve(b, n)
                        pe.wait_ge(v_dve if on_dve else v_act, v_count(b, n, on_dve))
                    if i < 2:
                        pe.wait_ge(taken["z"], KT)
                    if i >= 2:
                        pe.wait_ge(scan_done, i - 1)
                    for k in range(KT):
                        last = nc.tensor.transpose(dbu_ps[i % 2][:, k * P:(k + 1) * P], v_buf[:, (b * N + n) % RV, k, c * P:(c + 1) * P], ident[:])
                    last.then_inc(dbu_ready, 1)
                elif what[0] == "start":
                    b = what[1]
                    pe.wait_ge(du_ready, nth("dt", C - 1, b))
                    for k in range(KT):
                        if b > 0:
                            pe.wait_ge(gated, KT * (b - 1) + k + 1)
                        for c in range(C):
                            nc.tensor.matmul(y_ps[k][:, c * P:(c + 1) * P], lhsT=du[:, c, k * P:(k + 1) * P], rhs=ident[:],
                                             is_transpose=True, start=(c == 0), stop=False, skip_group_check=True)
                elif what[0] == "sum":
                    b, n, c = what[1:]
                    i = unit_no(b, n, c)
                    pe.wait_ge(prod_ready, i + 1)
                    for k in range(KT):
                        last = nc.tensor.matmul(y_ps[k][:, c * P:(c + 1) * P], lhsT=prod[:, i % RP, k * P:(k + 1) * P],
                                                rhs=ident[:], is_transpose=True, start=False,
                                                stop=(n == N - 1 and c == C - 1), skip_group_check=True)
                    last.then_inc(sum_done, 1)

        def scale_by_b(eng, done, b, n, k):
            scale = bc_rows[:, b % 2, k, n:n + 1]
            src, dst = dtu_rows[:, b % 2, k, :], v_buf[:, (b * N + n) % RV, k, :]
            if eng is nc.scalar:
                op = nc.scalar.activation(dst, src, ACT.Copy, scale=scale)
            else:
                op = nc.vector.tensor_scalar(dst, src, scale, None, ALU.mult)
            if k == KT - 1:
                op.then_inc(done, 1)

        def next_v(b, n):
            return (b, n + 1) if n + 1 < N else (b + 1, 0)

        @block.scalar
        def _(act):
            act.dma_start(w_ada, ada_w).then_inc(loaded_ada_w, 16)
            act.wait_ge(loaded_c, 16)
            nc.scalar.activation(cond_s[:], cond[:], ACT.Silu).then_inc(cond_ready, 1)
            nc.scalar.preload_act_table_set("natural_log_exp_and_others")
            act.wait_ge(loaded_vec, 16)
            nc.scalar.activation(a_exp[:], vec[:, at["a_log"]:at["a_log"] + C * N], ACT.Exp).then_inc(a_exp_ready, 1)

            def stage(kind, j, b):
                if kind == "silu_u":
                    for c in range(C):
                        act.wait_ge(taken["in"], nth("in", c, b))
                        last = nc.scalar.activation(u[:, c, :], u[:, c, :], ACT.Silu)
                    last.then_inc(u_ready, 1)
                    return
                if kind in ("silu_table", "exp_table"):
                    nc.scalar.preload_act_table_set("silu_and_others" if kind == "silu_table" else "natural_log_exp_and_others")
                    return
                ps = bank_of[kind, j, b]
                act.wait_ge(made[kind], nth(kind, j, b))
                if kind == "xt":
                    if b == 0 and j == 0:
                        act.wait_ge(mod_ready, 1)
                    if b > 1:
                        act.wait_ge(made["z"], nth("z", KT - 1, b - 2))
                    nc.scalar.activation(xn[:, b % 2, j, :], ps[:], ACT.Identity, scale=ln_scale[:, j, b:b + 1],
                                         bias=ln_shift[:, j, b:b + 1]).then_inc(taken["xt"], 1)
                elif kind == "in":
                    if b > 0:
                        act.wait_ge(sum_done, unit_no(b - 1, 0, 0) + 1)
                    w = at["conv_w"] + j * TAPS + TAPS - 1
                    nc.scalar.activation(u[:, j, :], ps[:], ACT.Identity, scale=vec[:, w:w + 1],
                                         bias=vec[:, at["conv_b"] + j:at["conv_b"] + j + 1]).then_inc(tap_ready, 1)
                elif kind == "z":
                    if b > 0:
                        act.wait_ge(gated, KT * b)
                    nc.scalar.activation(z_rows[:, j, :], ps[:], ACT.Silu).then_inc(taken["z"], 1)
                elif kind == "xp":
                    if b > 0:
                        act.wait_ge(made["dt"], nth("dt", C - 1, b - 1))
                        act.wait_ge(made["bct"], nth("bct", 0, b - 1))
                        act.wait_ge(c_stored, 16 * b)
                    nc.scalar.copy(dt_rank[0:R, :], ps[0:R, :])
                    nc.scalar.copy(bc[R:E_DBL, :], ps[R:E_DBL, :]).then_inc(taken["xp"], 1)
                elif kind == "dt":
                    i = b * C + j
                    if i >= 2:
                        act.wait_ge(dt_ready, i - 1)
                    nc.scalar.activation(soft[:, i % 2, :], ps[:], ACT.Abs).then_inc(sp_step, 1)
                    act.wait_ge(sp_step, 2 * i + 1)
                    nc.scalar.activation(soft[:, i % 2, :], soft[:, i % 2, :], ACT.Exp, scale=-1.0).then_inc(sp_step, 1)
                    act.wait_ge(sp_step, 2 * i + 2)
                    nc.scalar.activation(soft[:, i % 2, :], soft[:, i % 2, :], ACT.Ln, bias=1.0).then_inc(sp_ready, 1)
                elif kind == "bct":
                    if b >= 2:
                        act.wait_ge(v_dve, v_count(b - 2, N - 1, True))
                        act.wait_ge(v_act, v_count(b - 2, N - 1, False))
                    nc.scalar.copy(bc_rows[:, b % 2].rearrange("p k n -> p (k n)"), ps[:, 0:KT * 2 * N]).then_inc(taken["bct"], 1)
                elif kind == "du":
                    if b >= 2:
                        act.wait_ge(v_dve, v_count(b - 2, N - 1, True))
                        act.wait_ge(v_act, v_count(b - 2, N - 1, False))
                    nc.scalar.copy(dtu_rows[:, b % 2, j, :], ps[:]).then_inc(taken["du"], 1)
                elif kind == "yt":
                    if b > 0:
                        act.wait_ge(made["o"], nth("o", j, b - 1))
                    nc.scalar.copy(yg_cols[:, :, j * P:(j + 1) * P], ps[:].rearrange("p (c t) -> p c t", c=C)).then_inc(taken["yt"], 1)

            def v_waits(b, n):
                act.wait_ge(taken["bct"], b + 1)
                act.wait_ge(taken["du"], nth("du", KT - 1, b))
                if b * N + n >= RV:
                    act.wait_ge(dbu_ready, (b * N + n - RV + 1) * C)
                else:
                    act.wait_ge(ada_mm, 1)

            for what in work_of("act"):
                if what[0] != "unit":
                    stage(*what)
                elif what[0] == "unit":
                    b, n, c = what[1:]
                    i = unit_no(b, n, c)
                    if i == 0:
                        act.wait_ge(a_ready, 1)
                        act.wait_ge(dt_ready, C)
                    if n == 0 and c == 0:
                        act.wait_ge(dt_ready, nth("dt", C - 1, b))
                    if i >= RA:
                        act.wait_ge(scan_done, i - RA + 1)
                    nc.scalar.activation(d_a[:, i % RA, :], dt[:, b % 2, c, :], ACT.Exp,
                                         scale=a_neg[:, c * N + n:c * N + n + 1]).then_inc(da_ready, 1)
                    nb, nn = next_v(b, n)
                    if nb < BATCHES and not v_on_dve(nb, nn):
                        if c == 0:
                            v_waits(nb, nn)
                        scale_by_b(nc.scalar, v_act, nb, nn, c)

        @block.vector
        def _(dve):
            def modulation():
                dve.wait_ge(loaded_vec, 16)
                dve.wait_ge(ada_mm, 1)
                ab = vec[:, at["ada_b"]:at["ada_b"] + EA].unsqueeze(2).broadcast_to([P, EA, BATCHES])
                nc.vector.tensor_tensor(ada[:], dbu_ps[0][:, 0:EA * BATCHES].rearrange("p (m b) -> p m b", m=EA), ab,
                                        ALU.add).then_inc(mod_step, 1)
                dve.wait_ge(mod_step, 1)
                g = vec[:, at["ln_g"]:at["ln_g"] + DC].unsqueeze(2).broadcast_to([P, DC, BATCHES])
                lb = vec[:, at["ln_b"]:at["ln_b"] + DC].unsqueeze(2).broadcast_to([P, DC, BATCHES])
                scale, shift = ada[:, DC:2 * DC, :], ada[:, 0:DC, :]
                nc.vector.scalar_tensor_tensor(ln_scale[:], scale, 1.0, g, ALU.add, ALU.mult)
                nc.vector.scalar_tensor_tensor(ln_shift[:], scale, 1.0, lb, ALU.add, ALU.mult).then_inc(mod_step, 1)
                dve.wait_ge(mod_step, 2)
                nc.vector.tensor_tensor(ln_shift[:], ln_shift[:], shift, ALU.add).then_inc(mod_ready, 1)
                dve.wait_ge(a_exp_ready, 1)
                nc.vector.tensor_scalar(a_neg[:], a_exp[:], -1.0, None, ALU.mult).then_inc(a_ready, 1)

            def stage(kind, j, b, delay=0):
                if kind == "ada":
                    modulation()
                elif kind == "stats":
                    dve.wait_ge(loaded_x[b % 2], 16 * (b // 2 + 1))
                    for k in range(KT):
                        last = nc.vector.bn_stats(stats[:, k, :], x_sb[:, b % 2, k, :])
                    last.then_inc(ln_step, 1)
                    dve.wait_ge(ln_step, 3 * b + 1)
                    for k in range(KT):
                        last = nc.vector.bn_aggr(mean_var[:, k, :], stats[:, k, :])
                    last.then_inc(ln_step, 1)
                    dve.wait_ge(ln_step, 3 * b + 2)
                    nc.vector.tensor_scalar(var_eps[:], mean_var[:, :, 1], EPS, None, ALU.add).then_inc(ln_step, 1)
                elif kind == "xh":
                    dve.wait_ge(rstd_ready, b + 1)
                    if b > 0:
                        dve.wait_ge(made["xt"], nth("xt", DC - 1, b - 1))
                    for k in range(KT):
                        last = nc.vector.tensor_scalar(xh[:, k, :], x_sb[:, b % 2, k, :], mean_var[:, k, 0:1],
                                                       rstd[:, k:k + 1], ALU.subtract, ALU.mult)
                    last.then_inc(xh_ready, 1)
                elif kind == "tap":
                    ps = bank_of["in", j, b]
                    if delay == 1:
                        dve.wait_ge(tap_ready, nth("in", j, b))
                    else:
                        dve.wait_ge(conv_step, (TAPS - 2) * (b * C + j) + delay - 1)
                    w = at["conv_w"] + j * TAPS + TAPS - 1 - delay
                    nc.vector.scalar_tensor_tensor(u[:, j, delay:T], ps[:, 0:T - delay], vec[:, w:w + 1], u[:, j, delay:T],
                                                   ALU.mult, ALU.add).then_inc(taken["in"] if delay == TAPS - 1 else conv_step, 1)
                elif kind == "dt":
                    i = b * C + j
                    ps = bank_of[kind, j, b]
                    dve.wait_ge(sp_ready, i + 1)
                    if b >= 2 and j == 0:
                        dve.wait_ge(da_ready, unit_no(b - 2, N - 1, C - 1) + 1)
                    nc.vector.scalar_tensor_tensor(dt[:, b % 2, j, :], ps[:], 0.0, soft[:, i % 2, :], ALU.max,
                                                   ALU.add).then_inc(dt_ready, 1)
                elif kind == "dtu":
                    dve.wait_ge(dt_ready, nth("dt", j, b))
                    nc.vector.tensor_tensor(dtu[:, j, :], dt[:, b % 2, j, :], u[:, j, :], ALU.mult).then_inc(dtu_ready, 1)
                elif kind == "du":
                    dve.wait_ge(dtu_ready, nth("dt", j, b))
                    nc.vector.tensor_scalar(du[:, j, :], u[:, j, :], vec[:, at["d_param"] + j:at["d_param"] + j + 1], None,
                                            ALU.mult).then_inc(du_ready, 1)
                elif kind == "v":
                    dve.wait_ge(taken["bct"], 1)
                    dve.wait_ge(taken["du"], KT)
                    for k in range(KT):
                        scale_by_b(nc.vector, v_dve, 0, 0, k)
                elif kind == "o":
                    ps = bank_of[kind, j, b]
                    dve.wait_ge(made["o"], nth("o", j, b))
                    dve.wait_ge(loaded_xt, 16 * (b + 1))
                    if b > 0:
                        dve.wait_ge(out_stored, 16 * KT * b)
                    t = slice(j * P, (j + 1) * P)
                    for i in range(DC):
                        last = nc.vector.scalar_tensor_tensor(o_sb[:, i, t], ps[:, i * P:(i + 1) * P],
                                                              ada[:, 2 * DC + i, b:b + 1], xt_sb[:, i, t], ALU.mult, ALU.add)
                    last.then_inc(taken["o"], 1)

            for what in work_of("dve"):
                if what[0] not in ("unit", "gate"):
                    stage(*what)
                elif what[0] == "unit":
                    b, n, c = what[1:]
                    i = unit_no(b, n, c)
                    dve.wait_ge(dbu_ready, i + 1)
                    dve.wait_ge(da_ready, i + 1)
                    if i >= RH:
                        dve.wait_ge(prod_ready, i - RH + 1)
                    nc.vector.tensor_tensor_scan(h[:, i % RH, :], d_a[:, i % RA, :], dbu_ps[i % 2][:], 0.0, ALU.mult,
                                                 ALU.add).then_inc(scan_done, 1)
                    nb, nn = next_v(b, n)
                    if nb < BATCHES and v_on_dve(nb, nn):
                        if c == 0:
                            dve.wait_ge(taken["bct"], nb + 1)
                            dve.wait_ge(taken["du"], nth("du", KT - 1, nb))
                            if nb * N + nn >= RV:
                                dve.wait_ge(dbu_ready, (nb * N + nn - RV + 1) * C)
                            else:
                                dve.wait_ge(ada_mm, 1)
                        scale_by_b(nc.vector, v_dve, nb, nn, c)
                elif what[0] == "gate":
                    b = what[1]
                    dve.wait_ge(sum_done, U * (b + 1))
                    if b > 0:
                        dve.wait_ge(made["yt"], nth("yt", KT - 1, b - 1))
                    dve.wait_ge(taken["z"], nth("z", KT - 1, b))
                    for k in range(KT):
                        nc.vector.tensor_tensor(yg[:, k, :], y_ps[k][:], z_rows[:, k, :], ALU.mult).then_inc(gated, 1)


_INS = ["x_rows", "x_cols", "c_cols", "vectors", "ada_w", "in_x_w", "in_z_w", "x_proj_w", "dt_proj_w", "out_w"]


def kernel(**inputs):
    import numpy as np
    import concourse.bacc as bacc
    from concourse import mybir
    from concourse.bass_utils import run_bass_kernel_spmd

    w = {k.removeprefix("L0_cond_"): np.asarray(v) for k, v in inputs.items()}
    P = 128

    def chunks(a):
        return np.ascontiguousarray(np.moveaxis(a.reshape(a.shape[0] // P, P, *a.shape[1:]), 0, 1))

    x = w["x"]
    DI = w["in_proj_w"].shape[0] // 2
    names = ["ln_g", "ln_b", "ada_b", "conv_w", "conv_b", "D_param", "A_log"]
    laid = {
        "x_rows": x,
        "x_cols": x.transpose(0, 2, 1),
        "c_cols": chunks(w["cond_2048"].T),
        "vectors": np.concatenate([chunks(w[n]).reshape(P, -1) for n in names], axis=1),
        "ada_w": chunks(w["ada_w"].T),
        "in_x_w": chunks(w["in_proj_w"][:DI].T),
        "in_z_w": chunks(w["in_proj_w"][DI:].T),
        "x_proj_w": chunks(w["x_proj_w"].T),
        "dt_proj_w": np.concatenate([w["dt_proj_w"].T, w["dt_proj_b"][None, :]], axis=0),
        "out_w": chunks(w["out_proj_w"].T),
    }
    nc = bacc.Bacc("TRN2", target_bir_lowering=False, num_devices=1)
    arrays, args = {}, []
    for name in _INS:
        a = np.ascontiguousarray(laid[name])
        arrays[f"in_{name}"] = a
        args.append(nc.dram_tensor(f"in_{name}", a.shape, mybir.dt.from_np(a.dtype), kind="ExternalInput").ap())
    B, T, D = x.shape
    args.append(nc.dram_tensor("out_cols", (B, D, T), mybir.dt.float32, kind="ExternalOutput").ap())
    mamba_block(nc, *args)
    r = run_bass_kernel_spmd(nc, [arrays], core_ids=[0])
    return np.ascontiguousarray(r.results[0]["out_cols"].transpose(0, 2, 1))
```

```python
import concourse.bass as bass
from concourse import mybir
from contextlib import ExitStack


def mamba_block(nc, x_rows, x_cols, c_cols, vectors, ada_w, in_x_w, in_z_w, x_proj_w, dt_proj_w, out_w, out_cols):
    F32 = mybir.dt.float32
    ALU = mybir.AluOpType
    ACT = mybir.ActivationFunctionType

    P = 128
    BATCHES, T, D = x_rows.shape
    DC = D // P
    KT = T // P
    DI = in_x_w.shape[2]
    C = DI // P
    E_DBL = x_proj_w.shape[2]
    R = dt_proj_w.shape[0] - 1
    N = (E_DBL - R) // 2
    TAPS = 4
    CC = c_cols.shape[1]
    EA = ada_w.shape[2] // P
    EPS = 1e-5
    U = N * C

    at = {}
    col = 0
    for name, width in (("ln_g", DC), ("ln_b", DC), ("ada_b", EA), ("conv_w", C * TAPS), ("conv_b", C),
                        ("d_param", C), ("a_log", C * N)):
        at[name] = col
        col += width
    VCOLS = col

    LAG = 6
    RA, RH, RP = 6, 5, 8
    RV, RC = 3, 6
    DVE_V = (0, 0, 0, 0, 0, 0, 0, 4, 0, 4, 0, 0, 4, 0, 3, 0)
    SOFT = 4
    WARM_UP = 22
    S = BATCHES * N

    ctx = ExitStack()
    with ctx:
        def sb(name, shape, dt=F32):
            return ctx.enter_context(nc.sbuf_tensor(name, shape, dt))

        def sem(name):
            return ctx.enter_context(nc.semaphore(name))

        vec = sb("vec", [P, VCOLS])
        w_x = sb("w_x", [P, DC, DI])
        w_z = sb("w_z", [P, DC, DI])
        w_xp = sb("w_xp", [P, C, E_DBL])
        w_dt = sb("w_dt", [R + 1, DI])
        w_out = sb("w_out", [P, C, D])
        ident = sb("ident", [P, P])
        v_buf = sb("v_buf", [P, RV, KT, DI])
        w_ada = v_buf[:].rearrange("p a k d -> p (a k d)")[:, 0:CC * EA * P].rearrange("p (c e) -> p c e", c=CC)
        cond = sb("cond", [P, CC, BATCHES])
        cond_s = sb("cond_s", [P, CC, BATCHES])
        ada = sb("ada", [P, EA, BATCHES])
        ln_scale = sb("ln_scale", [P, DC, BATCHES])
        ln_shift = sb("ln_shift", [P, DC, BATCHES])
        pick_b = sb("pick_b", [P, P])
        a_exp = sb("a_exp", [P, C * N])
        a_neg = sb("a_neg", [P, C * N])
        x_sb = sb("x_sb", [P, 2, KT, D])
        xt_sb = sb("xt_sb", [P, DC, T])
        stats = sb("stats", [P, KT, 6])
        mean_var = sb("mean_var", [P, KT, 2])
        var_eps = sb("var_eps", [P, KT])
        minus_half = sb("minus_half", [P, KT])
        rstd = sb("rstd", [P, KT])
        xh = sb("xh", [P, KT, D])
        xn = sb("xn", [P, 2, DC, T])
        u = sb("u", [P, C, T])
        dt_rank = sb("dt_rank", [R + 1, T])
        bc = sb("bc", [P, T])
        soft = sb("soft", [P, SOFT, T])
        dt = sb("dt", [P, 2, C, T])
        dtu = sb("dtu", [P, C, T])
        dtu_rows = sb("dtu_rows", [P, 2, KT, DI])
        bc_rows = sb("bc_rows", [P, 2, KT, 2 * N])
        z_rows = sb("z_rows", [P, KT, DI])
        c_rep = sb("c_rep", [P, RC, T])
        d_a = sb("d_a", [P, RA, T])
        h = sb("h", [P, RH, T])
        prod = sb("prod", [P, RP, T])
        yg = sb("yg", [P, KT, DI])
        yg_cols = sb("yg_cols", [P, C, T])
        o_sb = sb("o_sb", [P, DC, T])

        c_dram = nc.dram_tensor("c_dram", [BATCHES, N, T], F32, kind="Internal").ap()

        y_ps = [ctx.enter_context(nc.psum_tensor(f"y_ps{k}", [P, DI], F32)) for k in range(KT)]
        dbu_ps = [ctx.enter_context(nc.psum_tensor(f"dbu_ps{i}", [P, T], F32)) for i in range(2)]
        work_ps = [ctx.enter_context(nc.psum_tensor(f"work_ps{i}", [P, T], F32)) for i in range(2)] + y_ps + dbu_ps

        loaded_c = sem("loaded_c")
        loaded_ada_w = [sem(f"loaded_ada_w{i}") for i in range(3)]
        loaded_w_x = sem("loaded_w_x")
        loaded_w_z = sem("loaded_w_z")
        loaded_w_xp = sem("loaded_w_xp")
        loaded_w_dt = sem("loaded_w_dt")
        loaded_w_out = sem("loaded_w_out")
        loaded_vec = sem("loaded_vec")
        loaded_x = [sem(f"loaded_x{i}") for i in range(2)]
        loaded_xt = sem("loaded_xt")
        c_stored = sem("c_stored")
        c_loaded = [sem(f"c_loaded{i}") for i in range(RC)]
        out_stored = sem("out_stored")
        pick_ready = sem("pick_ready")
        ident_zero = sem("ident_zero")
        ident_ready = sem("ident_ready")
        cond_ready = sem("cond_ready")
        ada_mm = sem("ada_mm")
        mod_step = sem("mod_step")
        mod_ready = sem("mod_ready")
        ada_read = sem("ada_read")
        a_exp_ready = sem("a_exp_ready")
        a_ready = sem("a_ready")
        KINDS = {"xt": DC, "in": C, "z": KT, "xp": 1, "dt": C, "bct": 1, "b_rep": 1, "du": KT, "yt": C, "o": DC}
        STEPS = {"in": DC, "z": DC, "xp": C, "o": C}
        made = {k: sem(f"{k}_made") for k in KINDS}
        taken = {k: sem(f"{k}_taken") for k in KINDS}
        dt_ready = taken["dt"]
        rank_ready = sem("rank_ready")
        ln_step = sem("ln_step")
        rstd_ready = sem("rstd_ready")
        xh_ready = sem("xh_ready")
        tap_ready = sem("tap_ready")
        conv_step = sem("conv_step")
        u_ready = sem("u_ready")
        abs_ready = sem("abs_ready")
        exp_ready = sem("exp_ready")
        sp_ready = sem("sp_ready")
        dtu_ready = sem("dtu_ready")
        du_ready = sem("du_ready")
        v_act = sem("v_act")
        v_dve = sem("v_dve")
        da_ready = sem("da_ready")
        dbu_ready = sem("dbu_ready")
        dbu_first = sem("dbu_first")
        scan_done = sem("scan_done")
        prod_ready = sem("prod_ready")
        sum_done = sem("sum_done")
        gated = sem("gated")

        order = []

        def put(pos, engine, *what):
            order.append((pos, len(order), engine, what))

        bank_of = {}
        AA = 2
        SILU = 22.4

        def put_stage(pos, bank, kind, j, b, behind=(("act", AA),)):
            bank_of[kind, j, b] = work_ps[bank]
            for step in range(STEPS.get(kind, 1)):
                put(pos - (STEPS.get(kind, 1) - 1 - step) * 0.9, "pe", kind, j, b, step)
            for engine, lag in behind:
                put(pos + lag, engine, kind, j, b)

        def soft_width(b):
            return 2 if b else 1

        def first_dbu_at(c):
            return -73.5 + 1.5 * (c >= C // 2) + 0.1 * c

        def first_prologue():
            put(-99, "dve", "stats", 0, 0)
            put(-98, "pool", "rstd", 0, 0)
            put(-97, "dve", "xh", 0, 0)
            put(-96, "pe", "ada", 0)
            put(-96, "pe", "ada", 1)
            put(-96, "dve", "mod")
            for i in range(DC):
                put_stage(-95 + 0.1 * i, i, "xt", i, 0, (("act", 0),))
            put(-94.5, "dve", "stats", 0, 1)
            put(-94, "pool", "rstd", 0, 1)
            put(-94, "dve", "xh", 0, 1)
            for i in range(DC):
                put_stage(-89.5 + 0.1 * i, i, "xt", i, 1, (("act", 3),))
            put(-74, "pe", "ada", 2)
            put(-72.95, "dve", "ada_gate")
            for c in range(C):
                on_pe = -90 + 2 * c
                put_stage(on_pe, 2 + c, "in", c, 0, (("act", 1),))
                for delay in range(1, TAPS):
                    put(on_pe + 1, "dve", "tap", c, 0, delay)
                put(on_pe + 3.5, "act", "silu_u", c, 0)
            for k in range(KT // 2):
                put_stage(-83 + k, k, "z", k, 0, (("act", 2.6),))
            put(-79, "act", "exp_table", 0, 0)
            put(-78.9, "act", "a_exp")
            put(-78.1, "dve", "a_neg")
            put_stage(-79, 7, "xp", 0, 0, (("dve", 0), ("sp", 0)))
            put_stage(-77.4, 0, "bct", 0, 0, (("act", 2.9),))
            put_stage(-77.3, 1, "b_rep", 0, 0, ())
            for c in range(C):
                on_pe = -78 + c
                put_stage(on_pe, 2 + c, "dt", c, 0, (("act", 0.4), ("dve", 1)))
                put(on_pe + 0.4, "act", "soft", c, 0)
                put(on_pe + 1, "dve", "dtu", c, 0)
                put(first_dbu_at(c), "dve", "first_dbu", c)
            for k in range(KT):
                put_stage(-73 + 0.1 * k, 2 + k, "du", k, 0, (("act", 0),))
            for c in range(C):
                put(-78.09, "dve", "du", c, 0)

        def prologue(front, b):
            if b > 1:
                put(front - 7.7, "dve", "stats", 0, b)
                put(front - 8.4, "pool", "rstd", 0, b)
                put(front - 2, "dve", "xh", 0, b)
                for i in range(DC):
                    put_stage(front + 0.7 * i, i % 2, "xt", i, b)
            for c in range(C):
                on_pe = front + (7.9 + 3.2 * c if b == 1 else 4.1 + 3.5 * c)
                put_stage(on_pe, c % 2, "in", c, b, (("act", 2),))
                for delay in range(1, TAPS):
                    put(on_pe + 2.5, "dve", "tap", c, b, delay)
            silu = front + SILU
            put(silu, "act", "silu_table", 0, b)
            put(silu + 0.2, "act", "silu_u", 0, b)
            put(silu + 0.4, "act", "exp_table", 0, b)
            put_stage(front + 26.7, 0, "xp", 0, b, (("act", AA), ("sp", 5)))
            put_stage(front + 29, 1, "bct", 0, b)
            for c in range(C):
                on_pe = front + (29.5, 31, 35.7, 37.2)[c]
                put_stage(on_pe, c % 2, "dt", c, b, (("act", 2), ("dve", 3 if c % 2 else 4)))
                if c % 2:
                    put(on_pe + 2.01, "act", "soft", c - 1, b)
                put(on_pe + 3.9, "pool", "dtu", c, b)
                put(front + 56.7 + c, "dve", "du", c, b)
            for k in range(KT):
                put_stage(front + (50, 52, 52.7, 57.8)[k], k % 2, "du", k, b, (("act", 2),))

        def z_stage(front, b):
            silu = front + (46 if b + 1 == BATCHES else SILU)
            for k in range(KT) if b else range(KT // 2, KT):
                put_stage(silu - (4.4, 2.2, 0.4, 0.1)[k], k % 2, "z", k, b, ())
                put(silu + (0.1 if k < 2 else 0.3), "act", "z", k, b)
            if b + 1 == BATCHES:
                put(silu, "act", "silu_table", 0, b)
                put(silu + 0.4, "act", "exp_table", 0, b)

        def epilogue(front, b):
            early = 35 if b + 2 == BATCHES else 0
            for c in range(C):
                put_stage(front + (41.5, 44.5, 45.3, 48)[c] - early, c % 2, "yt", c, b, (("act", 2),))
            for i in range(DC):
                put_stage(front + (58.1, 62)[i] - (36.5 if early else 0), i % 2, "o", i, b, (("dve", 1), ("sp", 2)))

        units = [(s // N, s % N, c) for s in range(S - 2) for c in range(C)]
        units += [(s // N, s % N, c) for c in range(C) for s in (S - 2, S - 1)]
        place = {unit: i for i, unit in enumerate(units)}

        def v_engine(s, k):
            return "dve" if s == 1 or k >= KT - DVE_V[s % N] else "act"

        first_prologue()
        for b in range(BATCHES):
            if b + 1 < BATCHES:
                prologue(b * U, b + 1)
            z_stage(b * U, b)
            if b > 0:
                epilogue(b * U, b - 1)
        for s in range(S):
            put(-1 if s < RC else (s - RC + 1) * C + 0.5, "sp", "load_c", s // N, s % N)
        for i, (b, n, c) in enumerate(units):
            lag = LAG if i < len(units) - 2 * C else LAG + 1
            for engine in ("act", "pe", "dve", "pool"):
                put(i if i >= C else first_dbu_at(i), engine, "unit", b, n, c)
            if n == 0:
                put(i + LAG, "pe", "start", b, c)
            put(i + lag, "pe", "sum", b, n, c)
            if n == N - 1:
                put((S * C + (-1.98, -1.55, 0.1, 0.2)[c] if b == BATCHES - 1 else i + lag + 0.1), "dve", "gate", b, c)
                if b == BATCHES - 1:
                    put_stage(i + lag + 2.6, 2 + c, "yt", c, b, (("act", 8),))
                    for k in range(DC):
                        bank_of["o", k, b] = work_ps[k]
                        put(i + lag + 5.2, "pe", "o", k, b, c)
        for i in range(DC):
            put(S * C + 9, "dve", "o", i, BATCHES - 1)
            put(S * C + 9, "sp", "o", i, BATCHES - 1)
        for s in range(1, S):
            b, n = s // N, s % N
            for k in range(KT):
                engine = v_engine(s, k)
                ahead = {"act": -1, "dve": -2}[engine]
                put((s - 1) * C + k + ahead - (0.9 if s == S - 1 else 0) if s > 1 else -72.9 + 0.1 * k, engine, "v", b, n, k)
        order.sort(key=lambda o: o[:2])

        def work_of(engine):
            return [what for _, _, e, what in order if e == engine]

        before = {}
        last = [None] * len(work_ps)
        for what in work_of("pe"):
            if what[0] in KINDS and what[3] == 0:
                key = what[:3]
                bank = work_ps.index(bank_of[key])
                before[key], last[bank] = last[bank], key

        def du_of(b):
            return u if b else yg_cols

        def nth(kind, j, b):
            return b * KINDS[kind] + j + 1

        def unit_no(b, n, c):
            return place[b, n, c]

        def v_slot(s):
            return (s + RV - 1) % RV

        v_ready = {"act": v_act, "dve": v_dve}

        def v_count(s, engine):
            return sum(v_engine(i, k) == engine for i in range(1, s + 1) for k in range(KT))

        def dbu_count(i):
            return i + 1 - C

        block = ctx.enter_context(nc.Block())

        def scale_by_b(eng, done, b, n, k):
            scale = bc_rows[:, b % 2, k, n:n + 1]
            src, dst = dtu_rows[:, b % 2, k, :], v_buf[:, v_slot(b * N + n), k, :]
            if eng is nc.scalar:
                op = nc.scalar.activation(dst, src, ACT.Copy, scale=scale)
            else:
                op = nc.vector.tensor_scalar(dst, src, scale, None, ALU.mult)
            op.then_inc(done, 1)

        def b_scaling(eng, on, b, n, k):
            s = b * N + n
            on.wait_ge(taken["du"], nth("du", k, b))
            if k == 0 or v_engine(s, k) != v_engine(s, k - 1):
                on.wait_ge(taken["bct"], b + 1)
                if s > RV:
                    on.wait_ge(dbu_ready, dbu_count((s - RV + 1) * C - 1))
                elif s == RV:
                    on.wait_ge(scan_done, C)
                else:
                    on.wait_ge(ada_mm, 3)
            scale_by_b(eng, v_ready[v_engine(s, k)], b, n, k)

        @block.sync
        def _(sp):
            sp.dma_start(cond[:], c_cols).then_inc(loaded_c, 16)
            sp.dma_start(x_sb[:, 0], x_rows[0].rearrange("(k p) d -> p k d", p=P)).then_inc(loaded_x[0], 16)
            for part in range(2):
                own = slice(part * D, (part + 1) * D)
                sp.dma_start(w_ada[:, :, own], ada_w[:, :, own]).then_inc(loaded_ada_w[part], 16)
            sp.dma_start(vec[:], vectors).then_inc(loaded_vec, 16)
            sp.dma_start(w_x[:], in_x_w).then_inc(loaded_w_x, 16)
            sp.dma_start(x_sb[:, 1], x_rows[1].rearrange("(k p) d -> p k d", p=P)).then_inc(loaded_x[1], 16)
            sp.dma_start(w_ada[:, :, 2 * D:], ada_w[:, :, 2 * D:]).then_inc(loaded_ada_w[2], 16)
            sp.dma_start(w_xp[:], x_proj_w).then_inc(loaded_w_xp, 16)
            sp.dma_start(w_dt[:], dt_proj_w).then_inc(loaded_w_dt, 16)
            sp.dma_start(w_z[:], in_z_w).then_inc(loaded_w_z, 16)
            sp.dma_start(w_out[:], out_w).then_inc(loaded_w_out, 16)
            sp.dma_start(xt_sb[:], x_cols[0].rearrange("(i p) t -> p i t", p=P)).then_inc(loaded_xt, 16)
            for what in work_of("sp"):
                if what[0] == "xp":
                    b = what[2]
                    sp.wait_ge(taken["xp"], b + 1)
                    sp.dma_start(c_dram[b], bc[R + N:R + 2 * N, :]).then_inc(c_stored, 16)
                    if b + 2 < BATCHES:
                        sp.wait_ge(xh_ready, b + 1)
                        sp.dma_start(x_sb[:, b % 2], x_rows[b + 2].rearrange("(k p) d -> p k d", p=P)).then_inc(loaded_x[b % 2], 16)
                elif what[0] == "load_c":
                    b, n = what[1:]
                    s = b * N + n
                    sp.wait_ge(c_stored, 16 * (b + 1))
                    if s >= RC:
                        sp.wait_ge(prod_ready, (s - RC + 1) * C)
                    sp.dma_start(c_rep[:, s % RC, :], c_dram[b, n:n + 1, :].broadcast_to([P, T])).then_inc(c_loaded[s % RC], 16)
                elif what[0] == "o":
                    k, b = what[1:]
                    sp.wait_ge(taken["o"], nth("o", k, b))
                    sp.dma_start(out_cols[b, k * P:(k + 1) * P, :], o_sb[:, k, :]).then_inc(out_stored, 16)
                    if k == DC - 1 and b + 1 < BATCHES:
                        sp.dma_start(xt_sb[:], x_cols[b + 1].rearrange("(i p) t -> p i t", p=P)).then_inc(loaded_xt, 16)
            sp.wait_ge(c_stored, 16 * BATCHES)
            sp.wait_ge(out_stored, 16 * DC * BATCHES)

        @block.gpsimd
        def _(pool):
            nc.gpsimd.memset(ident[:], 0.0).then_inc(ident_zero, 1)
            pool.wait_ge(ident_zero, 1)
            nc.gpsimd.affine_select(out=ident[:], in_=ident[:], compare_op=ALU.not_equal, fill=1.0, base=0,
                                    pattern=[[-1, P]], channel_multiplier=1).then_inc(ident_ready, 1)
            nc.gpsimd.memset(minus_half[:], -0.5).then_inc(ident_ready, 1)
            pool.wait_ge(ident_ready, 2)
            nc.gpsimd.memset(dt_rank[R:R + 1, :], 1.0).then_inc(ident_ready, 1)
            pool.wait_ge(ident_ready, 3)
            for what in work_of("pool"):
                if what[0] == "unit":
                    b, n, c = what[1:]
                    i = unit_no(b, n, c)
                    s = b * N + n
                    if c == 0:
                        pool.wait_ge(c_loaded[s % RC], 16 * (s // RC + 1))
                    pool.wait_ge(scan_done, i + 1)
                    if i >= RP:
                        pool.wait_ge(sum_done, i - RP + 1)
                    nc.gpsimd.tensor_tensor(prod[:, i % RP, :], h[:, i % RH, :], c_rep[:, s % RC, :], ALU.mult).then_inc(prod_ready, 1)
                elif what[0] == "rstd":
                    b = what[2]
                    pool.wait_ge(ln_step, 3 * b + 3)
                    nc.gpsimd.tensor_tensor(rstd[:], var_eps[:], minus_half[:], ALU.pow).then_inc(rstd_ready, 1)
                elif what[0] == "dtu":
                    c, b = what[1:]
                    pool.wait_ge(dt_ready, nth("dt", c, b))
                    if b > 0:
                        pool.wait_ge(made["du"], nth("du", KT - 1, b - 1))
                    nc.gpsimd.tensor_tensor(dtu[:, c, :], dt[:, b % 2, c, :], u[:, c, :], ALU.mult).then_inc(dtu_ready, 1)

        @block.tensor
        def _(pe):
            pe.wait_ge(ident_ready, 3)
            for _ in range(WARM_UP):
                nc.tensor.transpose(work_ps[0][:, 0:P], ident[:], ident[:])

            def ada_products(part):
                for m in range(part * DC, (part + 1) * DC):
                    for k in range(CC):
                        op = nc.tensor.matmul(dbu_ps[1 if part < 2 else 0][:, m * BATCHES:(m + 1) * BATCHES],
                                              lhsT=w_ada[:, k, m * P:(m + 1) * P], rhs=cond_s[:, k, :],
                                              start=(k == 0), stop=(k == CC - 1))
                op.then_inc(ada_mm, 1)

            def stage(kind, j, b, step):
                ps = bank_of[kind, j, b]
                was = before[kind, j, b]
                first, final = step == 0, step == STEPS.get(kind, 1) - 1
                if first and was is not None:
                    if was[0] == "b_rep":
                        pe.wait_ge(dbu_first, C)
                    else:
                        pe.wait_ge(taken[was[0]], nth(*was))
                if kind == "xt":
                    pe.wait_ge(xh_ready, b + 1)
                    for k in range(KT):
                        last = nc.tensor.transpose(ps[:, k * P:(k + 1) * P], xh[:, k, j * P:(j + 1) * P], ident[:])
                elif kind == "in":
                    if first:
                        pe.wait_ge(loaded_w_x, 16)
                    pe.wait_ge(taken["xt"], nth("xt", step, b))
                    last = nc.tensor.matmul(ps[:], lhsT=w_x[:, step, j * P:(j + 1) * P], rhs=xn[:, b % 2, step, :],
                                            start=first, stop=final)
                elif kind == "z":
                    if first:
                        pe.wait_ge(loaded_w_z, 16)
                    last = nc.tensor.matmul(ps[:], lhsT=xn[:, b % 2, step, j * P:(j + 1) * P], rhs=w_z[:, step, :],
                                            start=first, stop=final)
                elif kind == "xp":
                    if first:
                        pe.wait_ge(loaded_w_xp, 16)
                    pe.wait_ge(u_ready, nth("in", step, b))
                    last = nc.tensor.matmul(ps[0:E_DBL, :], lhsT=w_xp[:, step, :], rhs=u[:, step, :], start=first, stop=final)
                elif kind == "dt":
                    pe.wait_ge(loaded_w_dt, 16)
                    pe.wait_ge(rank_ready, b + 1)
                    last = nc.tensor.matmul(ps[:], lhsT=w_dt[:, j * P:(j + 1) * P], rhs=dt_rank[:], start=True, stop=True)
                elif kind == "bct":
                    pe.wait_ge(taken["xp"], nth("xp", 0, b))
                    for k in range(KT):
                        last = nc.tensor.transpose(ps[:, k * 2 * N:(k + 1) * 2 * N], bc[R:E_DBL, k * P:(k + 1) * P],
                                                   ident[R:E_DBL, R:E_DBL])
                elif kind == "b_rep":
                    pe.wait_ge(pick_ready, 1)
                    last = nc.tensor.matmul(ps[:], lhsT=pick_b[R:E_DBL, :], rhs=bc[R:E_DBL, :], start=True, stop=True)
                elif kind == "du":
                    pe.wait_ge(dtu_ready, nth("dt", C - 1, b))
                    for c in range(C):
                        last = nc.tensor.transpose(ps[:, c * P:(c + 1) * P], dtu[:, c, j * P:(j + 1) * P], ident[:])
                elif kind == "yt":
                    pe.wait_ge(gated, nth("yt", j, b))
                    for k in range(KT):
                        last = nc.tensor.transpose(ps[:, k * P:(k + 1) * P], yg[:, k, j * P:(j + 1) * P], ident[:])
                elif kind == "o":
                    if first:
                        pe.wait_ge(loaded_w_out, 16)
                    pe.wait_ge(taken["yt"], nth("yt", step, b))
                    last = nc.tensor.matmul(ps[:], lhsT=w_out[:, step, j * P:(j + 1) * P], rhs=yg_cols[:, step, :],
                                            start=first, stop=final)
                if final:
                    last.then_inc(made[kind], 1)

            for what in work_of("pe"):
                if what[0] in KINDS:
                    stage(*what)
                elif what[0] == "ada":
                    pe.wait_ge(loaded_ada_w[what[1]], 16)
                    pe.wait_ge(cond_ready, 1)
                    ada_products(what[1])
                elif what[0] == "unit":
                    b, n, c = what[1:]
                    i = unit_no(b, n, c)
                    if i < C:
                        continue
                    if c == 0:
                        s = b * N + n
                        for engine in sorted({v_engine(s, k) for k in range(KT)}):
                            pe.wait_ge(v_ready[engine], v_count(s, engine))
                    if i < C + 2:
                        pe.wait_ge(ada_read, 1)
                        pe.wait_ge(taken["xp"], 1)
                    else:
                        pe.wait_ge(scan_done, i - 1)
                    for k in range(KT):
                        last = nc.tensor.transpose(dbu_ps[i % 2][:, k * P:(k + 1) * P],
                                                   v_buf[:, v_slot(b * N + n), k, c * P:(c + 1) * P], ident[:])
                    last.then_inc(dbu_ready, 1)
                elif what[0] == "start":
                    b, c = what[1:]
                    pe.wait_ge(du_ready, nth("dt", c, b))
                    if b == 0:
                        pe.wait_ge(taken["du"], nth("du", c, 0))
                    else:
                        pe.wait_ge(gated, C * (b - 1) + c + 1)
                    for k in range(KT):
                        nc.tensor.matmul(y_ps[c][:, k * P:(k + 1) * P], lhsT=du_of(b)[:, c, k * P:(k + 1) * P], rhs=ident[:],
                                         is_transpose=True, start=(k == 0), stop=False, skip_group_check=True)
                elif what[0] == "sum":
                    b, n, c = what[1:]
                    i = unit_no(b, n, c)
                    pe.wait_ge(prod_ready, i + 1)
                    for k in range(KT):
                        last = nc.tensor.matmul(y_ps[c][:, k * P:(k + 1) * P], lhsT=prod[:, i % RP, k * P:(k + 1) * P],
                                                rhs=ident[:], is_transpose=True, start=False,
                                                stop=(n == N - 1 and k == KT - 1), skip_group_check=True)
                    last.then_inc(sum_done, 1)

        @block.scalar
        def _(act):
            nc.scalar.preload_act_table_set("silu_and_others")
            act.wait_ge(loaded_c, 16)
            nc.scalar.activation(cond_s[:], cond[:], ACT.Silu).then_inc(cond_ready, 1)

            def stage(kind, j=0, b=0):
                if kind == "silu_u":
                    width = C if b else 1
                    act.wait_ge(taken["in"], nth("in", j + width - 1, b))
                    nc.scalar.activation(u[:, j:j + width, :], u[:, j:j + width, :], ACT.Silu).then_inc(u_ready, width)
                    return
                if kind == "a_exp":
                    nc.scalar.activation(a_exp[:], vec[:, at["a_log"]:at["a_log"] + C * N], ACT.Exp).then_inc(a_exp_ready, 1)
                    return
                if kind in ("silu_table", "exp_table"):
                    nc.scalar.preload_act_table_set("silu_and_others" if kind == "silu_table" else "natural_log_exp_and_others")
                    return
                if kind == "soft":
                    width = soft_width(b)
                    i = b * C + j
                    both = soft[:, i % SOFT:i % SOFT + width, :]
                    act.wait_ge(abs_ready, i + width)
                    nc.scalar.activation(both, both, ACT.Exp, scale=-1.0).then_inc(exp_ready, width)
                    act.wait_ge(exp_ready, i + width)
                    nc.scalar.activation(both, both, ACT.Ln, bias=1.0).then_inc(sp_ready, width)
                    return
                ps = bank_of[kind, j, b]
                act.wait_ge(made[kind], nth(kind, j, b))
                if kind == "xt":
                    if b == 0 and j == 0:
                        act.wait_ge(mod_ready, 1)
                    if b > 1:
                        act.wait_ge(made["z"], nth("z", KT - 1, b - 2))
                    nc.scalar.activation(xn[:, b % 2, j, :], ps[:], ACT.Identity, scale=ln_scale[:, j, b:b + 1],
                                         bias=ln_shift[:, j, b:b + 1]).then_inc(taken["xt"], 1)
                elif kind == "in":
                    if b > 0:
                        act.wait_ge(sum_done, unit_no(b - 1, 0, j) + 1)
                    w = at["conv_w"] + j * TAPS + TAPS - 1
                    nc.scalar.activation(u[:, j, :], ps[:], ACT.Identity, scale=vec[:, w:w + 1],
                                         bias=vec[:, at["conv_b"] + j:at["conv_b"] + j + 1]).then_inc(tap_ready, 1)
                elif kind == "z":
                    if b > 0:
                        act.wait_ge(gated, C * b)
                    nc.scalar.activation(z_rows[:, j, :], ps[:], ACT.Silu).then_inc(taken["z"], 1)
                elif kind == "xp":
                    if b > 0:
                        act.wait_ge(made["dt"], nth("dt", C - 1, b - 1))
                        act.wait_ge(made["bct"], nth("bct", 0, b - 1))
                        act.wait_ge(c_stored, 16 * b)
                    nc.scalar.copy(dt_rank[0:R, :], ps[0:R, :]).then_inc(rank_ready, 1)
                    nc.scalar.copy(bc[R:E_DBL, :], ps[R:E_DBL, :]).then_inc(taken["xp"], 1)
                elif kind == "dt":
                    i = b * C + j
                    if i >= SOFT:
                        act.wait_ge(dt_ready, i - SOFT + 1)
                    nc.scalar.activation(soft[:, i % SOFT, :], ps[:], ACT.Abs).then_inc(abs_ready, 1)
                elif kind == "bct":
                    if b >= 2:
                        for engine in ("act", "dve"):
                            act.wait_ge(v_ready[engine], v_count((b - 1) * N - 1, engine))
                    nc.scalar.copy(bc_rows[:, b % 2].rearrange("p k n -> p (k n)"), ps[:, 0:KT * 2 * N]).then_inc(taken["bct"], 1)
                elif kind == "du":
                    if b >= 2:
                        for engine in ("act", "dve"):
                            act.wait_ge(v_ready[engine], v_count((b - 1) * N - 1, engine))
                    nc.scalar.copy(dtu_rows[:, b % 2, j, :], ps[:]).then_inc(taken["du"], 1)
                elif kind == "yt":
                    if b > 0:
                        act.wait_ge(made["o"], nth("o", DC - 1, b - 1))
                    nc.scalar.copy(yg_cols[:, j, :], ps[:]).then_inc(taken["yt"], 1)

            for what in work_of("act"):
                if what[0] == "v":
                    b_scaling(nc.scalar, act, *what[1:])
                elif what[0] != "unit":
                    stage(*what)
                else:
                    b, n, c = what[1:]
                    i = unit_no(b, n, c)
                    if i == 0:
                        act.wait_ge(a_ready, 1)
                    if n == 0:
                        act.wait_ge(dt_ready, nth("dt", c, b))
                    if i >= RA:
                        act.wait_ge(scan_done, i - RA + 1)
                    nc.scalar.activation(d_a[:, i % RA, :], dt[:, b % 2, c, :], ACT.Exp,
                                         scale=a_neg[:, c * N + n:c * N + n + 1]).then_inc(da_ready, 1)

        @block.vector
        def _(dve):
            mod_ps, gate_ps = (ps[:, 0:EA * BATCHES].rearrange("p (m b) -> p m b", m=EA) for ps in (dbu_ps[1], dbu_ps[0]))

            def spread(name, lo, width):
                return vec[:, at[name] + lo:at[name] + lo + width].unsqueeze(2).broadcast_to([P, width, BATCHES])

            def stage(kind, j=0, b=0, delay=0):
                if kind == "mod":
                    dve.wait_ge(loaded_vec, 16)
                    dve.wait_ge(ada_mm, 2)
                    nc.vector.tensor_tensor(ada[:, 0:2 * DC, :], mod_ps[:, 0:2 * DC, :], spread("ada_b", 0, 2 * DC),
                                            ALU.add).then_inc(mod_step, 1)
                    dve.wait_ge(mod_step, 1)
                    shift, scale = ada[:, 0:DC, :], ada[:, DC:2 * DC, :]
                    nc.vector.scalar_tensor_tensor(ln_scale[:], scale, 1.0, spread("ln_g", 0, DC), ALU.add, ALU.mult)
                    nc.vector.scalar_tensor_tensor(ln_shift[:], scale, 1.0, spread("ln_b", 0, DC), ALU.add,
                                                   ALU.mult).then_inc(mod_step, 1)
                    dve.wait_ge(mod_step, 2)
                    nc.vector.tensor_tensor(ln_shift[:], ln_shift[:], shift, ALU.add).then_inc(mod_ready, 1)
                elif kind == "ada_gate":
                    dve.wait_ge(ada_mm, 3)
                    nc.vector.tensor_tensor(ada[:, 2 * DC:, :], gate_ps[:, 2 * DC:, :], spread("ada_b", 2 * DC, DC),
                                            ALU.add).then_inc(ada_read, 1)
                elif kind == "a_neg":
                    dve.wait_ge(a_exp_ready, 1)
                    nc.vector.tensor_scalar(a_neg[:], a_exp[:], -1.0, None, ALU.mult).then_inc(a_ready, 1)
                elif kind == "xp":
                    ps = bank_of[kind, j, b]
                    dve.wait_ge(made["xp"], 1)
                    dve.wait_ge(ident_ready, 3)
                    nc.vector.tensor_copy(dt_rank[0:R, :], ps[0:R, :]).then_inc(rank_ready, 1)
                    nc.vector.tensor_copy(bc[R:E_DBL, :], ps[R:E_DBL, :]).then_inc(taken["xp"], 1)
                elif kind == "first_dbu":
                    dve.wait_ge(made["b_rep"], 1)
                    dve.wait_ge(dtu_ready, j + 1)
                    nc.vector.tensor_tensor(v_buf[:, v_slot(0), j, :], dtu[:, j, :], bank_of["b_rep", 0, 0][:],
                                            ALU.mult).then_inc(dbu_first, 1)
                elif kind == "stats":
                    dve.wait_ge(loaded_x[b % 2], 16 * (b // 2 + 1))
                    for k in range(KT):
                        last = nc.vector.bn_stats(stats[:, k, :], x_sb[:, b % 2, k, :])
                    last.then_inc(ln_step, 1)
                    dve.wait_ge(ln_step, 3 * b + 1)
                    for k in range(KT):
                        last = nc.vector.bn_aggr(mean_var[:, k, :], stats[:, k, :])
                    last.then_inc(ln_step, 1)
                    dve.wait_ge(ln_step, 3 * b + 2)
                    nc.vector.tensor_scalar(var_eps[:], mean_var[:, :, 1], EPS, None, ALU.add).then_inc(ln_step, 1)
                elif kind == "xh":
                    dve.wait_ge(rstd_ready, b + 1)
                    if b > 0:
                        dve.wait_ge(made["xt"], nth("xt", DC - 1, b - 1))
                    for k in range(KT):
                        last = nc.vector.tensor_scalar(xh[:, k, :], x_sb[:, b % 2, k, :], mean_var[:, k, 0:1],
                                                       rstd[:, k:k + 1], ALU.subtract, ALU.mult)
                    last.then_inc(xh_ready, 1)
                elif kind == "tap":
                    ps = bank_of["in", j, b]
                    if delay == 1:
                        dve.wait_ge(tap_ready, nth("in", j, b))
                    else:
                        dve.wait_ge(conv_step, (TAPS - 2) * (b * C + j) + delay - 1)
                    w = at["conv_w"] + j * TAPS + TAPS - 1 - delay
                    nc.vector.scalar_tensor_tensor(u[:, j, delay:T], ps[:, 0:T - delay], vec[:, w:w + 1], u[:, j, delay:T],
                                                   ALU.mult, ALU.add).then_inc(taken["in"] if delay == TAPS - 1 else conv_step, 1)
                elif kind == "dt":
                    i = b * C + j
                    ps = bank_of[kind, j, b]
                    dve.wait_ge(sp_ready, i + 1)
                    if b >= 2 and j == 0:
                        dve.wait_ge(da_ready, unit_no(b - 2, N - 1, C - 1) + 1)
                    nc.vector.scalar_tensor_tensor(dt[:, b % 2, j, :], ps[:], 0.0, soft[:, i % SOFT, :], ALU.max,
                                                   ALU.add).then_inc(dt_ready, 1)
                elif kind == "dtu":
                    dve.wait_ge(dt_ready, nth("dt", j, b))
                    nc.vector.tensor_tensor(dtu[:, j, :], dt[:, b % 2, j, :], u[:, j, :], ALU.mult).then_inc(dtu_ready, 1)
                elif kind == "du":
                    if b > 0:
                        dve.wait_ge(dtu_ready, nth("dt", j, b))
                    nc.vector.tensor_scalar(du_of(b)[:, j, :], u[:, j, :], vec[:, at["d_param"] + j:at["d_param"] + j + 1], None,
                                            ALU.mult).then_inc(du_ready, 1)
                elif kind == "o":
                    ps = bank_of[kind, j, b]
                    dve.wait_ge(made["o"], nth("o", j, b))
                    dve.wait_ge(loaded_xt, 16 * (b + 1))
                    if b > 0:
                        dve.wait_ge(out_stored, 16 * DC * b)
                    nc.vector.scalar_tensor_tensor(o_sb[:, j, :], ps[:], ada[:, 2 * DC + j, b:b + 1], xt_sb[:, j, :], ALU.mult,
                                                   ALU.add).then_inc(taken["o"], 1)

            dve.wait_ge(ident_ready, 3)
            nc.vector.tensor_copy(pick_b[R:E_DBL, :], ident[R:E_DBL, R:R + 1].broadcast_to([2 * N, P])).then_inc(pick_ready, 1)
            for what in work_of("dve"):
                if what[0] == "v":
                    b_scaling(nc.vector, dve, *what[1:])
                elif what[0] == "unit":
                    b, n, c = what[1:]
                    i = unit_no(b, n, c)
                    if i < C:
                        dve.wait_ge(dbu_first, i + 1)
                    else:
                        dve.wait_ge(dbu_ready, dbu_count(i))
                    dve.wait_ge(da_ready, i + 1)
                    if i >= RH:
                        dve.wait_ge(prod_ready, i - RH + 1)
                    dbu = v_buf[:, v_slot(0), c, :] if i < C else dbu_ps[i % 2][:]
                    nc.vector.tensor_tensor_scan(h[:, i % RH, :], d_a[:, i % RA, :], dbu, 0.0, ALU.mult,
                                                 ALU.add).then_inc(scan_done, 1)
                elif what[0] == "gate":
                    b, c = what[1:]
                    dve.wait_ge(sum_done, unit_no(b, N - 1, c) + 1)
                    if b > 0:
                        dve.wait_ge(made["yt"], nth("yt", c, b - 1))
                    dve.wait_ge(taken["z"], nth("z", KT - 1, b))
                    own = slice(c * P, (c + 1) * P)
                    nc.vector.tensor_tensor(yg[:, :, own], y_ps[c][:].rearrange("p (k d) -> p k d", k=KT), z_rows[:, :, own],
                                            ALU.mult).then_inc(gated, 1)
                else:
                    stage(*what)


_INS = ["x_rows", "x_cols", "c_cols", "vectors", "ada_w", "in_x_w", "in_z_w", "x_proj_w", "dt_proj_w", "out_w"]


def kernel(**inputs):
    import numpy as np
    import concourse.bacc as bacc
    from concourse import mybir
    from concourse.bass_utils import run_bass_kernel_spmd

    w = {k.removeprefix("L0_cond_"): np.asarray(v) for k, v in inputs.items()}
    P = 128

    def chunks(a):
        return np.ascontiguousarray(np.moveaxis(a.reshape(a.shape[0] // P, P, *a.shape[1:]), 0, 1))

    x = w["x"]
    DI = w["in_proj_w"].shape[0] // 2
    names = ["ln_g", "ln_b", "ada_b", "conv_w", "conv_b", "D_param", "A_log"]
    laid = {
        "x_rows": x,
        "x_cols": x.transpose(0, 2, 1),
        "c_cols": chunks(w["cond_2048"].T),
        "vectors": np.concatenate([chunks(w[n]).reshape(P, -1) for n in names], axis=1),
        "ada_w": chunks(w["ada_w"].T),
        "in_x_w": chunks(w["in_proj_w"][:DI].T),
        "in_z_w": chunks(w["in_proj_w"][DI:].T),
        "x_proj_w": chunks(w["x_proj_w"].T),
        "dt_proj_w": np.concatenate([w["dt_proj_w"].T, w["dt_proj_b"][None, :]], axis=0),
        "out_w": chunks(w["out_proj_w"].T),
    }
    nc = bacc.Bacc("TRN2", target_bir_lowering=False, num_devices=1)
    arrays, args = {}, []
    for name in _INS:
        a = np.ascontiguousarray(laid[name])
        arrays[f"in_{name}"] = a
        args.append(nc.dram_tensor(f"in_{name}", a.shape, mybir.dt.from_np(a.dtype), kind="ExternalInput").ap())
    B, T, D = x.shape
    args.append(nc.dram_tensor("out_cols", (B, D, T), mybir.dt.float32, kind="ExternalOutput").ap())
    mamba_block(nc, *args)
    r = run_bass_kernel_spmd(nc, [arrays], core_ids=[0])
    return np.ascontiguousarray(r.results[0]["out_cols"].transpose(0, 2, 1))
```
